# Optimizing a Trainium2 kernel written in Bass

```python
import numpy as np
import jax
import jax.numpy as jnp

def _softmax(x, axis=-1):
    return jax.nn.softmax(x, axis=axis)

def _gelu(x):
    return jax.nn.gelu(x, approximate=True)

def _silu(x):
    return jax.nn.silu(x)

def _sigmoid(x):
    return jax.nn.sigmoid(x)

def _layernorm(x, axis=-1, eps=1e-05):
    m = jnp.mean(x, axis=axis, keepdims=True)
    v = jnp.var(x, axis=axis, keepdims=True)
    return (x - m) / jnp.sqrt(v + eps)

def _scatter_add(tgt, idx, src, axis=0):
    return tgt.at[idx].add(src)

def _segment_sum(src, seg, n):
    return jax.ops.segment_sum(src, seg, n)
kernel_name = 'mk_gnn_preln_d2_gnn_r64_c3abbc'

def setup_inputs(seed: int=0):
    np.random.seed(seed)
    _w = jnp.asarray

    def _rec_inputs():
        import jax
        import jax.numpy as jnp
        _gk = jax.random.key(seed)
        x = -0.000202 + 1 * jax.random.normal(jax.random.fold_in(_gk, 1), (100000, 64), jnp.float32)
        src = jax.random.randint(jax.random.fold_in(_gk, 2), (25000,), 0, 100000, jnp.int32)
        dst = jax.random.randint(jax.random.fold_in(_gk, 3), (25000,), 0, 100000, jnp.int32)
        _o = jnp.argsort(dst, stable=True)
        src = src[_o]
        dst = dst[_o]
        edge_attr_32 = -5.3897e-05 + 0.999841 * jax.random.normal(jax.random.fold_in(_gk, 11), (25000, 32), jnp.float32)
        return (x, src, dst, edge_attr_32)
    x, src, dst, edge_attr_32 = _rec_inputs()

    def _L0_gnn_setup():
        import jax, jax.numpy as jnp
        import numpy as np
        N_NODES = 100000
        NEG_SLOPE = 0.2
        EPS = 1e-16
        key = jax.random.key(seed)
        k1, k2, k3, k4 = jax.random.split(key, 4)
        in_dim, out_dim, n_edges = (64, 64, 25000)
        x = jax.random.normal(k1, (N_NODES, in_dim), dtype=jnp.float32)
        edge_index = jax.random.randint(k2, (2, n_edges), 0, N_NODES, dtype=jnp.int64)
        W = jax.random.normal(k3, (in_dim, out_dim), dtype=jnp.float32) / np.sqrt(in_dim)
        ka, kb = jax.random.split(k4)
        att_src = jax.random.normal(ka, (out_dim,), dtype=jnp.float32) / np.sqrt(out_dim)
        att_dst = jax.random.normal(kb, (out_dim,), dtype=jnp.float32) / np.sqrt(out_dim)
        bias = jnp.zeros((out_dim,), dtype=jnp.float32)
        return {'x': x, 'edge_index': edge_index, 'W': W, 'att_src': att_src, 'att_dst': att_dst, 'bias': bias}
    _L0_gnn_all = _L0_gnn_setup()
    _L0_gnn_in = {k: v for k, v in _L0_gnn_all.items() if k in ('W', 'att_src', 'att_dst', 'bias')}
    del _L0_gnn_all

    def _L1_gnn_setup():
        import jax, jax.numpy as jnp
        import numpy as np
        N_NODES = 50000
        N_EDGES = 12500
        D_NODE = 64
        D_EDGE = 32
        H_MSG = (2 * D_NODE + D_EDGE) // 2
        H_CMB = 3 * D_NODE // 2

        def _gelu(x):
            return jax.nn.gelu(x, approximate=False)
        key = jax.random.key(seed)
        ks = jax.random.split(key, 11)

        def lin(k, fan_in, fan_out):
            bound = 1.0 / np.sqrt(fan_in)
            k1, k2 = jax.random.split(k)
            W = jax.random.uniform(k1, (fan_in, fan_out), jnp.float32, -bound, bound)
            b = jax.random.uniform(k2, (fan_out,), jnp.float32, -bound, bound)
            return (W, b)
        node_vectors = jax.random.normal(ks[0], (N_NODES, D_NODE), jnp.float32)
        edge_vectors = jax.random.normal(ks[1], (N_EDGES, D_EDGE), jnp.float32)
        edge_indices = jax.random.randint(ks[2], (N_EDGES, 2), 0, N_NODES, jnp.int64 if jax.config.jax_enable_x64 else jnp.int32)
        W_m1, b_m1 = lin(ks[3], 2 * D_NODE + D_EDGE, H_MSG)
        W_m2, b_m2 = lin(ks[4], H_MSG, D_NODE)
        W_c1, b_c1 = lin(ks[5], 2 * D_NODE, H_CMB)
        W_c2, b_c2 = lin(ks[6], H_CMB, D_NODE)
        return {'node_vectors': node_vectors, 'edge_vectors': edge_vectors, 'edge_indices': edge_indices, 'W_m1': W_m1, 'b_m1': b_m1, 'W_m2': W_m2, 'b_m2': b_m2, 'W_c1': W_c1, 'b_c1': b_c1, 'W_c2': W_c2, 'b_c2': b_c2}
    _L1_gnn_all = _L1_gnn_setup()
    _L1_gnn_in = {k: v for k, v in _L1_gnn_all.items() if k in ('W_m1', 'b_m1', 'W_m2', 'b_m2', 'W_c1', 'b_c1', 'W_c2', 'b_c2')}
    del _L1_gnn_all
    return {'x': x, 'src': src, 'dst': dst, 'edge_attr_32': edge_attr_32, 'L0_gnn_W': _L0_gnn_in['W'], 'L0_gnn_att_src': _L0_gnn_in['att_src'], 'L0_gnn_att_dst': _L0_gnn_in['att_dst'], 'L0_gnn_bias': _L0_gnn_in['bias'], 'L1_gnn_W_m1': _L1_gnn_in['W_m1'], 'L1_gnn_b_m1': _L1_gnn_in['b_m1'], 'L1_gnn_W_m2': _L1_gnn_in['W_m2'], 'L1_gnn_b_m2': _L1_gnn_in['b_m2'], 'L1_gnn_W_c1': _L1_gnn_in['W_c1'], 'L1_gnn_b_c1': _L1_gnn_in['b_c1'], 'L1_gnn_W_c2': _L1_gnn_in['W_c2'], 'L1_gnn_b_c2': _L1_gnn_in['b_c2']}

def reference(x, src, dst, edge_attr_32, L0_gnn_W, L0_gnn_att_src, L0_gnn_att_dst, L0_gnn_bias, L1_gnn_W_m1, L1_gnn_b_m1, L1_gnn_W_m2, L1_gnn_b_m2, L1_gnn_W_c1, L1_gnn_b_c1, L1_gnn_W_c2, L1_gnn_b_c2):
    import jax
    import jax.numpy as jnp

    def _L0_gnn_ref(x, edge_index, W, att_src, att_dst, bias):
        import jax, jax.numpy as jnp
        import numpy as np
        N_NODES = 100000
        NEG_SLOPE = 0.2
        EPS = 1e-16
        src, dst = (edge_index[0], edge_index[1])
        h = x @ W
        a_src = h @ att_src
        a_dst = h @ att_dst
        e = jax.nn.leaky_relu(a_src[src] + a_dst[dst], NEG_SLOPE)
        m = jax.ops.segment_max(e, dst, num_segments=N_NODES)
        e = jnp.exp(e - m[dst])
        denom = jax.ops.segment_sum(e, dst, num_segments=N_NODES)
        alpha = e / (denom[dst] + EPS)
        out = jax.ops.segment_sum(alpha[:, None] * h[src], dst, num_segments=N_NODES)
        return jnp.tanh(out + bias)

    def _L1_gnn_ref(node_vectors, edge_vectors, edge_indices, W_m1, b_m1, W_m2, b_m2, W_c1, b_c1, W_c2, b_c2):
        import jax, jax.numpy as jnp
        import numpy as np
        N_NODES = 50000
        N_EDGES = 12500
        D_NODE = 64
        D_EDGE = 32
        H_MSG = (2 * D_NODE + D_EDGE) // 2
        H_CMB = 3 * D_NODE // 2

        def _gelu(x):
            return jax.nn.gelu(x, approximate=False)
        node_i = node_vectors[edge_indices[:, 0]]
        node_j = node_vectors[edge_indices[:, 1]]
        msg_input = jnp.concatenate([node_i, node_j, edge_vectors], axis=1)
        h = _gelu(msg_input @ W_m1 + b_m1)
        messages = _gelu(h @ W_m2 + b_m2)
        boxes = jax.ops.segment_sum(messages, edge_indices[:, 1], num_segments=node_vectors.shape[0])
        pairs = jnp.concatenate([node_vectors, boxes], axis=1)
        c = _gelu(pairs @ W_c1 + b_c1)
        combined = _gelu(c @ W_c2 + b_c2)
        return node_vectors + combined
    edge_index = jnp.stack([src, dst])
    edge_index_t = jnp.stack([src, dst], axis=1)
    h = jnp.maximum(_layernorm(x, axis=-1), 0.0)
    x = x + _L0_gnn_ref(h, edge_index, L0_gnn_W, L0_gnn_att_src, L0_gnn_att_dst, L0_gnn_bias)
    h = jnp.maximum(_layernorm(x, axis=-1), 0.0)
    x = x + _L1_gnn_ref(h, edge_attr_32, edge_index_t, L1_gnn_W_m1, L1_gnn_b_m1, L1_gnn_W_m2, L1_gnn_b_m2, L1_gnn_W_c1, L1_gnn_b_c1, L1_gnn_W_c2, L1_gnn_b_c2)
    return x

_drawn_inputs = setup_inputs


def setup_inputs(seed=0):
    import zlib

    import numpy as np

    out = dict(_drawn_inputs(seed))
    spreads = {'L0_gnn_bias': (0.0, 0.1)}
    factors = {'edge_attr_32': 8.0,
     'L0_gnn_att_src': 18.434,
     'L0_gnn_att_dst': 64.0,
     'L1_gnn_W_m1': 8.0,
     'L1_gnn_b_m1': 22.126,
     'L1_gnn_W_m2': 8.0,
     'L1_gnn_b_m2': 52.949,
     'L1_gnn_b_c1': 8.0,
     'L1_gnn_b_c2': 3.106}
    for name, (base, spread) in spreads.items():
        noise = np.random.default_rng([zlib.crc32(name.encode()), seed]).standard_normal(out[name].shape)
        drawn = base * np.exp(spread * noise) if base else spread * noise
        out[name] = jnp.asarray(drawn.astype(out[name].dtype))
    for name, factor in factors.items():
        out[name] = (out[name] * factor).astype(out[name].dtype)
    return out
```

```python
import concourse.bass as bass
from concourse import mybir
from contextlib import ExitStack


def gnn_two_layer_kernel(
    nc: bass.Bass,
    x: bass.AP,
    src: bass.AP,
    dst: bass.AP,
    edge_attr: bass.AP,
    W0: bass.AP,
    att_src: bass.AP,
    att_dst: bass.AP,
    bias0: bass.AP,
    W_m1: bass.AP,
    b_m1: bass.AP,
    W_m2: bass.AP,
    b_m2: bass.AP,
    W_c1: bass.AP,
    b_c1: bass.AP,
    W_c2: bass.AP,
    b_c2: bass.AP,
    out: bass.AP,
):
    fp32 = mybir.dt.float32
    i32 = mybir.dt.int32
    ALU = mybir.AluOpType
    ACT = mybir.ActivationFunctionType
    AX = mybir.AxisListType
    ds = bass.ds

    N, D = x.shape
    E = src.shape[0]
    DE = edge_attr.shape[1]
    HM = W_m1.shape[1]
    HC = W_c1.shape[1]
    P = 125
    ET = E // P
    TE = 4
    UNITS = ET // TE
    UE = TE * P
    TN = N // UNITS // P
    UN = TN * P
    GE = 2 * TE
    RB = 2
    RR = ET // RB
    PM = 120
    LN_EPS = 1e-5
    SM_EPS = 1e-16
    SLOPE = 0.2
    BIG = 1.0e30
    SKIP = float(1 << 20)
    D1 = D + 1
    TRIPS = UNITS // 2
    assert E == ET * P and ET == UNITS * TE and N == UNITS * UN and UNITS % 2 == 0

    node_table = nc.dram_tensor("node_table", [N, D], fp32).ap()
    decay_dram = nc.dram_tensor("decay_dram", [E], fp32).ap()
    same_dram = nc.dram_tensor("same_dram", [E], fp32).ap()

    def known(u, least):
        return not isinstance(u, int) or u >= least

    def mirror(i, s):
        return i * -2 + (UNITS - 1 - s)

    def bcast(ap, shape, axis):
        return ap.unsqueeze(axis).broadcast_to(shape)

    def rows_of(dram):
        return dram.rearrange("(b r p) -> r b p", b=RB, p=P)

    ctx = ExitStack()
    first_phase = ExitStack()
    with ctx:
        scope = [ctx]

        def sb(name, shape, dt=fp32):
            return scope[0].enter_context(nc.sbuf_tensor(name, shape, dt))

        def sem(name):
            return ctx.enter_context(nc.semaphore(name))

        def two(name, shape, dt=fp32):
            return [sb(f"{name}{s}", shape, dt) for s in range(2)]

        ident = sb("ident", [128, 128])
        stack_id = sb("stack_id", [128, D])
        w0_ext = sb("w0_ext", [D1, D1])
        w0_t = sb("w0_t", [D, D])
        att_col = sb("att_col", [D, 2])
        att_rep = sb("att_rep", [D, 2, 128])
        att_vec = sb("att_vec", [P, GE, D])
        tanh_b = sb("tanh_b", [P, D])
        wc1_top = sb("wc1_top", [128, HC])
        wc1_box = sb("wc1_box", [D, HC])
        wc2_ext = sb("wc2_ext", [HC + 1, D])
        wm1_dst = sb("wm1_dst", [D, HM])
        wm1_src = sb("wm1_src", [D + DE, HM])
        wm2 = sb("wm2", [HM, D])
        bc1 = sb("bc1", [HC, 1])
        bm1 = sb("bm1", [HM, 1])
        bm2 = sb("bm2", [D, 1])
        row_dst = sb("row_dst", [RR, RB, P + 2], i32)
        row_src = sb("row_src", [RR, RB, P], i32)
        row_dst_f = sb("row_dst_f", [RR, RB, P + 2])
        row_src_f = sb("row_src_f", [RR, RB, P])
        same_prev = sb("same_prev", [RR, RB, P])
        same_next = sb("same_next", [RR, RB, P])
        gather_idx = sb("gather_idx", [P, UNITS, GE], i32)
        dst_f = sb("dst_f", [P, ET])
        last_f = sb("last_f", [P, ET])
        first_f = sb("first_f", [P, ET])
        tmp_l = sb("tmp_l", [P, ET])
        tmp_f = sb("tmp_f", [P, ET])
        last_idx = sb("last_idx", [P, ET], i32)
        first_idx = sb("first_idx", [P, ET], i32)
        keep = sb("keep", [P, ET, 2 * D])
        logit = sb("logit", [P, ET])
        weight = sb("weight", [P, ET])
        scope[0] = first_phase
        idx_now = two("idx_now", [P, GE], i32)
        xe = two("xe", [P, GE, D])
        e_sum = sb("e_sum", [P, GE])
        e_mean = two("e_mean", [P, GE])
        e_cen = two("e_cen", [P, GE, D])
        e_sq = sb("e_sq", [P, GE, D])
        e_hdst = sb("e_hdst", [P, TE, D])
        e_prod = sb("e_prod", [P, GE, D])
        e_dot = sb("e_dot", [P, GE])
        xn = two("xn", [P, TN, D])
        x1n = two("x1n", [P, TN, D])
        n_sum = sb("n_sum", [P, TN])
        n_mean = two("n_mean", [P, TN])
        n_sq = sb("n_sq", [P, TN, D])
        h1n = two("h1n", [P, TN, D])
        s1n = two("s1n", [P, TN, D])
        h1t = sb("h1t", [128, 2, 4 * P])
        c1t = sb("c1t", [HC + 1, 4, 4 * P])
        resn = two("resn", [P, TN, D])
        var = sb("var", [P, 2, TN + GE])
        var_eps = sb("var_eps", [P, 2, TN + GE])
        std = sb("std", [P, 2, TN + GE])
        rstd = sb("rstd", [P, 2, TN + GE])
        pen = sb("pen", [RR, RB, P])
        pen_min = sb("pen_min", [RR, RB])
        z_row = sb("z_row", [RR, RB, P])
        e_row = sb("e_row", [RR, RB, P])
        m_row = sb("m_row", [RR, RB, P])
        m_run = sb("m_run", [RR, RB, P + 1])
        line = sb("line", [1, 2 * ET])
        line_m = sb("line_m", [1, ET + 1])
        d_row = sb("d_row", [RR, RB, P])
        decay_row = sb("decay_row", [RR, RB, P])
        w_row = sb("w_row", [RR, RB, P])
        first_phase.close()
        scope[0] = ctx
        wh = sb("wh", [P, 2 * TE, D1])
        decay = two("decay", [D1, UE])
        acc = two("acc", [D1, UE])
        lidx = two("lidx", [P, TE], i32)
        x_last = sb("x_last", [P, 2 * TE, D])
        den_eps = sb("den_eps", [P, 2 * TE])
        den_inv = sb("den_inv", [P, 2 * TE])
        den_last = sb("den_last", [P, 2 * TE])
        att_out = sb("att_out", [P, 2 * TE, D])
        x1_last = sb("x1_last", [P, 2 * TE, D])
        att_th = sb("att_th", [P, 2 * TE, D])
        l_sum = sb("l_sum", [P, 2 * TE])
        l_mean = sb("l_mean", [P, 2 * TE])
        l_cen = sb("l_cen", [P, 2 * TE, D])
        l_sq = sb("l_sq", [P, 2 * TE, D])
        l_var = sb("l_var", [P, 2 * TE])
        l_eps = sb("l_eps", [P, 2 * TE])
        l_std = sb("l_std", [P, 2 * TE])
        l_rstd = sb("l_rstd", [P, 2 * TE])
        h1e = two("h1e", [P, TE, D])
        sidx = two("sidx", [P, TE], i32)
        fidx = two("fidx", [P, TE], i32)
        cat = two("cat", [P, TE, D + DE])
        kept = two("kept", [P, TE, 2 * D])
        cat_t = sb("cat_t", [D + DE, UE])
        same = two("same", [128, UE])
        fill = two("fill", [128, UE])
        msg_h = sb("msg_h", [HM, UE])
        msg = sb("msg", [D, UE])
        box = two("box", [D, UE])
        c1e = sb("c1e", [HC + 1, UE])
        g3 = sb("g3", [P, TE, D])
        res = two("res", [P, TE, D])

        psum_all = ctx.enter_context(nc.psum_tensor("psum_all", [128, 8, 512], fp32))
        psum = [psum_all[:, i, :] for i in range(8)]

        d_pad = sem("d_pad")
        sp_turn = sem("sp_turn")
        pool_turn = sem("pool_turn")
        d_rows = sem("d_rows")
        d_w = sem("d_w")
        ident_z = sem("ident_z")
        ident_ok = sem("ident_ok")
        c_step = sem("c_step")
        c_pe = sem("c_pe")
        c_act = sem("c_act")
        nx_out = sem("nx_out")
        tables = sem("tables")
        idx_ok = sem("idx_ok")
        d_xe = [sem(f"d_xe{s}") for s in range(2)]
        esum_ok = sem("esum_ok")
        emean_ok = sem("emean_ok")
        ecen_ok = sem("ecen_ok")
        esq_ok = sem("esq_ok")
        evar_ok = sem("evar_ok")
        vareps_ok = sem("vareps_ok")
        std_ok = sem("std_ok")
        rstd_ok = sem("rstd_ok")
        eh_ok = sem("eh_ok")
        eprod_ok = sem("eprod_ok")
        edot_ok = sem("edot_ok")
        logit_ok = sem("logit_ok")
        xdst_ok = sem("xdst_ok")
        d_xn = [sem(f"d_xn{s}") for s in range(2)]
        nx1_ok = sem("nx1_ok")
        nsum_ok = sem("nsum_ok")
        nmean_ok = sem("nmean_ok")
        ncen_ok = sem("ncen_ok")
        nsq_ok = sem("nsq_ok")
        nvar_ok = sem("nvar_ok")
        h1n_ok = sem("h1n_ok")
        s1n_ok = sem("s1n_ok")
        h1t_ps = sem("h1t_ps")
        h1t_ok = sem("h1t_ok")
        c1_ps = sem("c1_ps")
        c1_ok = sem("c1_ok")
        z2_ps = sem("z2_ps")
        g2_ok = sem("g2_ok")
        resn_ok = sem("resn_ok")
        d_tab = [sem(f"d_tab{s}") for s in range(2)]
        d_res = [sem(f"d_res{s}") for s in range(2)]
        m_step = sem("m_step")
        m_pe = sem("m_pe")
        m_act = sem("m_act")
        d_flow = sem("d_flow")

        p1_done = sem("p1_done")
        p2_ready = sem("p2_ready")
        wh_ok = sem("wh_ok")
        whw_ok = sem("whw_ok")
        wht_ps = sem("wht_ps")
        d_dec = [sem(f"d_dec{s}") for s in range(2)]
        acc_ok = sem("acc_ok")
        num_ps = sem("num_ps")
        xlast_ok = sem("xlast_ok")
        dene_ok = sem("dene_ok")
        deni_ok = sem("deni_ok")
        denl_ok = sem("denl_ok")
        att_ok = sem("att_ok")
        th_ok = sem("th_ok")
        x1_ok = sem("x1_ok")
        x1k_ok = sem("x1k_ok")
        lsum_ok = sem("lsum_ok")
        lmean_ok = sem("lmean_ok")
        lcen_ok = sem("lcen_ok")
        lsq_ok = sem("lsq_ok")
        lvar_ok = sem("lvar_ok")
        leps_ok = sem("leps_ok")
        lstd_ok = sem("lstd_ok")
        lrstd_ok = sem("lrstd_ok")
        h1e_ok = sem("h1e_ok")
        h1k_ok = sem("h1k_ok")
        lidx_ok = sem("lidx_ok")
        d_sc = [sem(f"d_sc{s}") for s in range(2)]
        p2_done = sem("p2_done")
        sidx_ok = sem("sidx_ok")
        fidx_ok = sem("fidx_ok")
        d_cat = [sem(f"d_cat{s}") for s in range(2)]
        d_ea = [sem(f"d_ea{s}") for s in range(2)]
        d_same = [sem(f"d_same{s}") for s in range(2)]
        kept_ok = sem("kept_ok")
        catt_ps = sem("catt_ps")
        catt_ok = sem("catt_ok")
        keptt_ps = sem("keptt_ps")
        fill_ok = sem("fill_ok")
        m1_ps = sem("m1_ps")
        m1_ok = sem("m1_ok")
        m2_ps = sem("m2_ps")
        m2_ok = sem("m2_ok")
        box_ok = sem("box_ok")
        ce_ps = sem("ce_ps")
        ce_ok = sem("ce_ok")
        ge_ps = sem("ge_ps")
        ge_ok = sem("ge_ok")
        res_ok = sem("res_ok")
        d_fin = [sem(f"d_fin{s}") for s in range(2)]

        block = ctx.enter_context(nc.Block())

        def trips(eng, trip):
            trip(0)
            with eng.Fori(1, TRIPS) as i:
                trip(i)

        @block.sync
        def _(sp):
            with nc.allow_non_contiguous_dma(reason="one neighbour per row of 125 destinations"):
                sp.wait_ge(d_pad, 1)
                sp.dma_start(row_dst[:, :, 1:P + 1], rows_of(dst)).then_inc(d_rows, 16)
                sp.dma_start(row_src[:, :, :], rows_of(src)).then_inc(d_rows, 16)
                before = dst[P - 1:E].rearrange("(t o) -> t o", o=1)
                after = dst[P:E].rearrange("(t o) -> t o", o=1)
                for b in range(RB):
                    lo = 1 if b == 0 else 0
                    hi = RR if b < RB - 1 else RR - 1
                    t0 = b * RR + lo - 1
                    sp.dma_start(row_dst[lo:RR, b, 0:1],
                                 before[P * t0:P * (t0 + RR - lo - 1) + 1:P, :]).then_inc(d_rows, 16)
                    sp.dma_start(row_dst[0:hi, b, P + 1:P + 2],
                                 after[P * b * RR:P * (b * RR + hi - 1) + 1:P, :]).then_inc(d_rows, 16)
            for to, frm in (
                (w0_ext[0:D, 0:D], W0), (w0_ext[D:D1, 0:D], bias0.unsqueeze(0)),
                (att_col[:, 0:1], att_src.unsqueeze(1)), (att_col[:, 1:2], att_dst.unsqueeze(1)),
                (tanh_b[:, :], bias0.partition_broadcast(P)),
                (wc1_top[0:D, :], W_c1[0:D, :]), (wc1_top[D:2 * D, :], W_c1[0:D, :]),
                (wc1_box[:, :], W_c1[D:2 * D, :]),
                (wc2_ext[0:HC, :], W_c2), (wc2_ext[HC:HC + 1, :], b_c2.unsqueeze(0)),
                (wm1_src[0:D, :], W_m1[0:D, :]), (wm1_dst[:, :], W_m1[D:2 * D, :]),
                (wm1_src[D:D + DE, :], W_m1[2 * D:2 * D + DE, :]), (wm2[:, :], W_m2),
                (bc1[:, :], b_c1.unsqueeze(1)), (bm1[:, :], b_m1.unsqueeze(1)), (bm2[:, :], b_m2.unsqueeze(1)),
            ):
                sp.dma_start(to, frm).then_inc(d_w, 16)

            def nodes(dram, u):
                return dram[ds(u * UN, UN), :].rearrange("(p j) d -> p j d", j=TN)

            def load(u, s):
                for a, b in ((0, PM), (PM, P)):
                    sp.dma_start(xn[s][a:b, :, :], nodes(x, u)[a:b]).then_inc(d_xn[s], 16)

            load(0, 0)
            load(1, 1)

            def store_table(u, s):
                sp.wait_ge(h1n_ok, u + 1)
                for a, b in ((0, PM), (PM, P)):
                    sp.dma_start(nodes(node_table, u)[a:b], h1n[s][a:b, :, :]).then_inc(d_tab[s], 16)

            def store_result(u, s):
                sp.wait_ge(resn_ok, u + 1)
                for a, b in ((0, PM), (PM, P)):
                    sp.dma_start(nodes(out, u)[a:b], resn[s][a:b, :, :]).then_inc(d_res[s], 16)

            def p1(i):
                for s in range(2):
                    if not (isinstance(i, int) and i == TRIPS - 1):
                        sp.wait_ge(nx1_ok, 2 * i + s + 1)
                        load(2 * i + s + 2, s)
                for s in range(2):
                    if known(i, 1):
                        store_result(2 * i + s - 2, s)
                for s in range(2):
                    store_table(2 * i + s, s)

            p1(0)
            with sp.Fori(1, TRIPS - 1) as i:
                p1(i)
            p1(TRIPS - 1)
            for s in range(2):
                store_result(UNITS - 2 + s, s)

            sp.dma_start(rows_of(same_dram), same_next[:, :, :]).then_inc(d_flow, 16)
            sp.wait_ge(m_step, DECAY_READY)
            sp.dma_start(rows_of(decay_dram), decay_row[:, :, :]).then_inc(d_flow, 16)
            sp.wait_ge(d_flow, 32)
            for s in range(2):
                sp.wait_ge(d_tab[s], 32 * TRIPS)
                sp.wait_ge(d_res[s], 32 * TRIPS)
            sp.wait_ge(m_step, SM_DONE)
            sp.sem_inc(p1_done)

            def load_decay(u, s):
                sp.dma_start(decay[s][:, :], decay_dram[ds(u * UE, UE)].partition_broadcast(D1)).then_inc(d_dec[s], 16)

            def p2(i):
                for s in range(2):
                    u = 2 * i + s
                    if known(u, 2):
                        sp.wait_ge(acc_ok, u - 1)
                        sp.sem_inc(sp_turn)
                    load_decay(u, s)

            trips(sp, p2)

            def load_edges(i, s):
                e0 = mirror(i, s) * UE
                sp.dma_start(same[s][:, :], same_dram[ds(e0, UE)].partition_broadcast(128)).then_inc(d_same[s], 16)
                sp.dma_start(cat[s][:, :, D:D + DE], edge_attr[ds(e0, UE), :].rearrange("(j p) d -> p j d", p=P))\
                    .then_inc(d_ea[s], 16)

            def p3(i):
                for s in range(2):
                    v = 2 * i + s
                    if known(v, 2):
                        sp.wait_ge(box_ok, v - 1)
                        sp.wait_ge(catt_ps, v - 1)
                        sp.sem_inc(sp_turn)
                    load_edges(i, s)

            trips(sp, p3)

        @block.gpsimd
        def _(pool):
            pool.memset(row_dst[:, :, :], -1).then_inc(d_pad, 1)
            pool.memset(ident[:, :], 0.0).then_inc(ident_z, 1)
            pool.wait_ge(ident_z, 1)
            pool.affine_select(out=ident[:, :], in_=ident[:, :], compare_op=ALU.not_equal, fill=1.0,
                               base=0, pattern=[[-1, 128]], channel_multiplier=1).then_inc(ident_ok, 1)

            last_node = pool.to_reg(N - 1)

            def p1(i):
                for s in range(2):
                    u = 2 * i + s
                    pool.wait_ge(idx_ok, u + 1)
                    if known(u, 2):
                        pool.wait_ge(ecen_ok, u - 1)
                        pool.wait_ge(xdst_ok, u - 1)
                    pool.sem_inc(pool_turn)
                    for g in range(GE):
                        pool.indirect_dma_start(
                            out=xe[s][:, g, :], out_offset=None, in_=x,
                            in_offset=bass.IndirectOffsetOnAxis(ap=idx_now[s][:, g:g + 1], axis=0),
                            bounds_check=last_node, oob_is_err=False).then_inc(d_xe[s], 16)

            trips(pool, p1)

            pool.wait_ge(p1_done, 1)

            def p2(i):
                for s in range(2):
                    u = 2 * i + s
                    pool.wait_ge(lidx_ok, u + 1)
                    pool.wait_ge(h1e_ok, u + 1)
                    pool.sem_inc(pool_turn)
                    for j in range(TE):
                        pool.indirect_dma_start(
                            out=node_table, out_offset=bass.IndirectOffsetOnAxis(ap=lidx[s][:, j:j + 1], axis=0),
                            in_=h1e[s][:, j, :], in_offset=None,
                            bounds_check=last_node, oob_is_err=False).then_inc(d_sc[s], 16)

            trips(pool, p2)
            for s in range(2):
                pool.wait_ge(d_sc[s], 16 * TE * TRIPS)
            pool.sem_inc(p2_done)

            def gather(v, s):
                pool.wait_ge(sidx_ok, v + 1)
                if known(v, 2):
                    pool.wait_ge(catt_ps, v - 1)
                pool.sem_inc(pool_turn)
                for j in range(TE):
                    pool.indirect_dma_start(
                        out=cat[s][:, j, 0:D], out_offset=None, in_=node_table,
                        in_offset=bass.IndirectOffsetOnAxis(ap=sidx[s][:, j:j + 1], axis=0),
                        bounds_check=last_node, oob_is_err=False).then_inc(d_cat[s], 16)

            def scatter(v, s):
                pool.wait_ge(fidx_ok, v + 1)
                pool.wait_ge(res_ok, v + 1)
                pool.sem_inc(pool_turn)
                for j in range(TE):
                    pool.indirect_dma_start(
                        out=out, out_offset=bass.IndirectOffsetOnAxis(ap=fidx[s][:, j:j + 1], axis=0),
                        in_=res[s][:, j, :], in_offset=None,
                        bounds_check=last_node, oob_is_err=False).then_inc(d_fin[s], 16)

            gather(0, 0)
            gather(1, 1)

            def p3(i):
                for s in range(2):
                    v = 2 * i + s
                    if not (isinstance(i, int) and i == TRIPS - 1):
                        gather(v + 2, s)
                    if known(v, 1):
                        scatter(v - 1, 1 - s)

            p3(0)
            with pool.Fori(1, TRIPS - 1) as i:
                p3(i)
            p3(TRIPS - 1)
            scatter(UNITS - 1, 1)
            for s in range(2):
                pool.wait_ge(d_fin[s], 16 * TE * TRIPS)

        @block.scalar
        def _(act):
            act.wait_ge(d_w, 16 * 17)
            act.activation(tanh_b[:, :], tanh_b[:, :], ACT.Tanh).then_inc(c_act, 1)

            def squares(i, s):
                u = 2 * i + s
                act.wait_ge(ncen_ok, u + 1)
                if known(u, 1):
                    act.wait_ge(nvar_ok, u)
                act.activation(n_sq[:, :, :], h1n[s][:, :, :], ACT.Square, scale=D ** -0.5).then_inc(nsq_ok, 1)
                act.wait_ge(ecen_ok, u + 1)
                if known(u, 1):
                    act.wait_ge(evar_ok, u)
                act.activation(e_sq[:, :, :], e_cen[s][:, :, :], ACT.Square, scale=D ** -0.5).then_inc(esq_ok, 1)
                act.activation(keep[:, ds(u * TE, TE), D:2 * D], xe[s][:, TE:GE, :], ACT.Copy).then_inc(xdst_ok, 1)

            def evacuate(u):
                act.wait_ge(h1t_ps, u + 1)
                if known(u, 1):
                    act.wait_ge(c1_ps, 4 * u)
                act.activation(h1t[:, 0, :], psum[0][:, 0:4 * P], ACT.Copy).then_inc(h1t_ok, 1)
                act.activation(h1t[:, 1, :], psum[1][:, 0:4 * P], ACT.Copy).then_inc(h1t_ok, 1)

            def gelu_hidden(u):
                for q in range(4):
                    act.wait_ge(c1_ps, 4 * u + q + 1)
                    if q % 2 == 0 and known(u, 1):
                        act.wait_ge(z2_ps, 2 * u - 1 + q // 2)
                    act.activation(c1t[0:HC, q, :], psum[2 + q][0:HC, 0:4 * P], ACT.Gelu,
                                   bias=bc1[:, 0:1]).then_inc(c1_ok, 1)

            def gelu_out(u, s):
                for h in range(2):
                    act.wait_ge(z2_ps, 2 * u + h + 1)
                    if h == 0 and known(u, 2):
                        act.wait_ge(d_res[s], 16 * (u - s))
                    act.activation(resn[s][:, 8 * h:8 * h + 8, :],
                                   psum[6 + h][0:P, :].rearrange("p (j d) -> p j d", d=D),
                                   ACT.Gelu).then_inc(g2_ok, 1)

            def p1(i):
                squares(i, 0)
                squares(i, 1)
                if known(i, 1):
                    gelu_out(2 * i - 1, 1)
                act.wait_ge(vareps_ok, i + 1)
                act.activation(std[:, :, :], var_eps[:, :, :], ACT.Sqrt).then_inc(std_ok, 1)
                evacuate(2 * i)
                gelu_hidden(2 * i)
                evacuate(2 * i + 1)
                gelu_out(2 * i, 0)
                gelu_hidden(2 * i + 1)

            trips(act, p1)
            gelu_out(UNITS - 1, 1)

            act.wait_ge(m_step, DIFF_READY)
            act.activation(decay_row[:, :, :], d_row[:, :, :], ACT.Exp).then_inc(m_act, 1)
            act.activation(w_row[:, :, :], z_row[:, :, :], ACT.Exp).then_inc(m_act, 1)

            act.wait_ge(p1_done, 1)

            def p2(i):
                act.wait_ge(att_ok, i + 1)
                if known(i, 1):
                    act.wait_ge(x1_ok, i)
                act.activation(att_th[:, :, :], att_out[:, :, :], ACT.Tanh).then_inc(th_ok, 1)
                act.wait_ge(lcen_ok, i + 1)
                if known(i, 1):
                    act.wait_ge(lvar_ok, i)
                act.activation(l_sq[:, :, :], l_cen[:, :, :], ACT.Square, scale=D ** -0.5).then_inc(lsq_ok, 1)
                act.wait_ge(leps_ok, i + 1)
                if known(i, 1):
                    act.wait_ge(lrstd_ok, i)
                act.activation(keep[:, ds(i * 2 * TE, 2 * TE), D:2 * D], x1_last[:, :, :], ACT.Copy).then_inc(x1k_ok, 1)
                act.activation(l_std[:, :], l_eps[:, :], ACT.Sqrt).then_inc(lstd_ok, 1)
                for s in range(2):
                    u = 2 * i + s
                    act.wait_ge(h1e_ok, u + 1)
                    act.activation(keep[:, ds(u * TE, TE), 0:D], h1e[s][:, :, :], ACT.Copy).then_inc(h1k_ok, 1)

            trips(act, p2)

            def keep_copy(i, s):
                v = 2 * i + s
                if known(v, 2):
                    act.wait_ge(keptt_ps, v - 1)
                act.activation(kept[s][:, :, :], keep[:, ds(mirror(i, s) * TE, TE), :], ACT.Copy).then_inc(kept_ok, 1)

            def gelu_hidden_e(v):
                act.wait_ge(ce_ps, v + 1)
                if known(v, 1):
                    act.wait_ge(ge_ps, v)
                act.activation(c1e[0:HC, :], psum[5][0:HC, 0:UE], ACT.Gelu, bias=bc1[:, 0:1]).then_inc(ce_ok, 1)

            def gelu_out_e(v):
                act.wait_ge(ge_ps, v + 1)
                if known(v, 1):
                    act.wait_ge(res_ok, v)
                act.activation(g3[:, :, :], psum[6][0:P, 0:TE * D].rearrange("p (j d) -> p j d", d=D), ACT.Gelu)\
                    .then_inc(ge_ok, 1)

            act.wait_ge(h1k_ok, UNITS)
            act.wait_ge(x1k_ok, TRIPS)
            keep_copy(0, 0)

            def p3(i):
                for s in range(2):
                    v = 2 * i + s
                    act.wait_ge(catt_ps, v + 1)
                    if known(v, 1):
                        act.wait_ge(m1_ps, v)
                    act.activation(cat_t[:, :], psum[2][0:D + DE, 0:UE], ACT.Copy).then_inc(catt_ok, 1)
                    if known(v, 1):
                        gelu_hidden_e(v - 1)
                    act.wait_ge(m1_ps, v + 1)
                    if known(v, 1):
                        act.wait_ge(m2_ps, v)
                    act.activation(msg_h[:, :], psum[3][0:HM, 0:UE], ACT.Gelu, bias=bm1[:, 0:1]).then_inc(m1_ok, 1)
                    if known(v, 1):
                        gelu_out_e(v - 1)
                    if not (isinstance(i, int) and i == TRIPS - 1 and s == 1):
                        keep_copy(i + s, 1 - s)
                    act.wait_ge(m2_ps, v + 1)
                    if known(v, 1):
                        act.wait_ge(box_ok, v)
                    act.activation(msg[:, :], psum[4][0:D, 0:UE], ACT.Gelu, bias=bm2[:, 0:1]).then_inc(m2_ok, 1)

            p3(0)
            with act.Fori(1, TRIPS - 1) as i:
                p3(i)
            p3(TRIPS - 1)
            gelu_hidden_e(UNITS - 1)
            gelu_out_e(UNITS - 1)

        @block.vector
        def _(dve):
            step = [0]

            def then(ins):
                step[0] += 1
                ins.then_inc(c_step, 1)
                dve.wait_ge(c_step, step[0])

            dve.memset(w0_ext[:, D:D1], 0.0).then_inc(c_step, 1)
            step[0] += 1
            dve.wait_ge(c_step, 1)
            then(dve.memset(w0_ext[D:D1, D:D1], 1.0))
            then(dve.memset(line_m[0:1, 0:1], -BIG))
            then(dve.memset(c1t[HC:HC + 1, :, :], 1.0))
            dve.wait_ge(d_rows, 16 * (2 + 2 * RB))
            then(dve.tensor_copy(row_dst_f[:, :, :], row_dst[:, :, :]))
            then(dve.tensor_copy(row_src_f[:, :, :], row_src[:, :, :]))
            then(dve.tensor_tensor(same_prev[:, :, :], row_dst_f[:, :, 1:P + 1], row_dst_f[:, :, 0:P], ALU.is_equal))
            then(dve.tensor_tensor(same_next[:, :, :], row_dst_f[:, :, 1:P + 1], row_dst_f[:, :, 2:P + 2], ALU.is_equal))
            assert step[0] == ROWS_READY
            then(dve.tensor_scalar(pen[:, :, :], same_prev[:, :, :], -1.0, BIG, ALU.add, ALU.mult))
            then(dve.tensor_reduce(pen_min[:, :], pen[:, :, :], AX.X, ALU.min))
            dve.wait_ge(c_pe, 1)
            idx_v = gather_idx[:, :, :]
            then(dve.tensor_copy(idx_v[:, :, 0:TE], psum[0][0:P, 0:ET].rearrange("p (u j) -> p u j", j=TE)))
            then(dve.tensor_copy(idx_v[:, :, TE:GE], psum[0][0:P, 256:256 + ET].rearrange("p (u j) -> p u j", j=TE)))

            def stage_idx(u, s):
                dve.tensor_copy(idx_now[s][:, :], gather_idx[:, ds(u, 1), :].rearrange("p a g -> p (a g)"))\
                    .then_inc(idx_ok, 1)

            stage_idx(0, 0)
            stage_idx(1, 1)
            then(dve.tensor_copy(dst_f[:, :], psum[0][0:P, 256:256 + ET]))
            for psum_at, flag, tmp, idx in ((256, last_f, tmp_l, last_idx), (0, first_f, tmp_f, first_idx)):
                then(dve.tensor_scalar(flag[:, :], psum[1][0:P, psum_at:psum_at + ET], -1.0, 1.0, ALU.mult, ALU.add))
                then(dve.tensor_scalar(tmp[:, :], dst_f[:, :], -SKIP, None, ALU.add))
                then(dve.tensor_tensor(tmp[:, :], tmp[:, :], flag[:, :], ALU.mult))
                then(dve.tensor_scalar(idx[:, :], tmp[:, :], SKIP, None, ALU.add))
            dve.wait_ge(ident_ok, 1)
            then(dve.tensor_tensor(stack_id[:, :], ident[:, 0:D], ident[:, D:2 * D], ALU.add))
            dve.wait_ge(c_pe, 2)
            dve.wait_ge(d_w, 16 * 17)
            then(dve.tensor_copy(w0_t[:, :], psum[2][0:D, 0:D]))
            then(dve.tensor_copy(att_rep[:, :, :], bcast(att_col[:, :], [D, 2, 128], 2)))
            assert step[0] == ATT_READY
            dve.wait_ge(c_pe, 3)
            for g in range(2):
                then(dve.tensor_copy(att_vec[:, g * TE:(g + 1) * TE, :],
                                     bcast(psum[2][0:P, 64 + g * D:64 + (g + 1) * D], [P, TE, D], 1)))
            dve.wait_ge(c_act, 1)

            def means(i, s):
                u = 2 * i + s
                dve.wait_ge(d_xe[s], 16 * GE * (i + 1))
                dve.tensor_reduce(e_sum[:, :], xe[s][:, :, :], AX.X, ALU.add).then_inc(esum_ok, 1)
                dve.wait_ge(d_xn[s], 32 * (i + 1))
                if known(u, 2):
                    dve.wait_ge(s1n_ok, u - 1)
                dve.tensor_tensor(x1n[s][:, :, :], xn[s][:, :, :], bcast(tanh_b[:, :], [P, TN, D], 1),
                                  ALU.add).then_inc(nx1_ok, 1)
                dve.wait_ge(nx1_ok, u + 1)
                dve.tensor_reduce(n_sum[:, :], x1n[s][:, :, :], AX.X, ALU.add).then_inc(nsum_ok, 1)
                dve.wait_ge(nsum_ok, u + 1)
                dve.tensor_scalar(n_mean[s][:, :], n_sum[:, :], 1.0 / D, None, ALU.mult).then_inc(nmean_ok, 1)
                dve.wait_ge(esum_ok, u + 1)
                dve.tensor_scalar(e_mean[s][:, :], e_sum[:, :], 1.0 / D, None, ALU.mult).then_inc(emean_ok, 1)

            def centre(i, s):
                u = 2 * i + s
                if known(u, 2):
                    dve.wait_ge(d_tab[s], 32 * i)
                    dve.wait_ge(h1t_ps, u - 1)
                dve.wait_ge(nmean_ok, u + 1)
                dve.tensor_tensor(h1n[s][:, :, :], x1n[s][:, :, :], bcast(n_mean[s][:, :], [P, TN, D], 2),
                                  ALU.subtract).then_inc(ncen_ok, 1)
                dve.wait_ge(emean_ok, u + 1)
                dve.tensor_tensor(e_cen[s][:, :, :], xe[s][:, :, :], bcast(e_mean[s][:, :], [P, GE, D], 2),
                                  ALU.subtract).then_inc(ecen_ok, 1)
                if not (isinstance(i, int) and i == TRIPS - 1):
                    stage_idx(u + 2, s)

            def variances(u, s):
                dve.wait_ge(nsq_ok, u + 1)
                dve.tensor_reduce(var[:, s, 0:TN], n_sq[:, :, :], AX.X, ALU.add).then_inc(nvar_ok, 1)
                dve.wait_ge(esq_ok, u + 1)
                dve.tensor_reduce(var[:, s, TN:], e_sq[:, :, :], AX.X, ALU.add).then_inc(evar_ok, 1)

            def normalise(i, s):
                u = 2 * i + s
                dve.scalar_tensor_tensor(out=h1n[s][:, :, :], in0=h1n[s][:, :, :], scalar=0.0,
                                         in1=bcast(rstd[:, s, 0:TN], [P, TN, D], 2),
                                         op0=ALU.max, op1=ALU.mult).then_inc(h1n_ok, 1)
                dve.scalar_tensor_tensor(out=keep[:, ds(u * TE, TE), 0:D], in0=e_cen[s][:, 0:TE, :], scalar=0.0,
                                         in1=bcast(rstd[:, s, TN:TN + TE], [P, TE, D], 2),
                                         op0=ALU.max, op1=ALU.mult).then_inc(eh_ok, 1)
                dve.scalar_tensor_tensor(out=e_hdst[:, :, :], in0=e_cen[s][:, TE:GE, :], scalar=0.0,
                                         in1=bcast(rstd[:, s, TN + TE:], [P, TE, D], 2),
                                         op0=ALU.max, op1=ALU.mult).then_inc(eh_ok, 1)
                dve.wait_ge(h1n_ok, u + 1)
                dve.tensor_tensor(s1n[s][:, :, :], x1n[s][:, :, :], h1n[s][:, :, :], ALU.add).then_inc(s1n_ok, 1)
                dve.wait_ge(eh_ok, 2 * u + 2)
                dve.tensor_tensor(e_prod[:, 0:TE, :], keep[:, ds(u * TE, TE), 0:D], att_vec[:, 0:TE, :],
                                  ALU.mult).then_inc(eprod_ok, 1)
                dve.tensor_tensor(e_prod[:, TE:GE, :], e_hdst[:, :, :], att_vec[:, TE:GE, :],
                                  ALU.mult).then_inc(eprod_ok, 1)
                dve.wait_ge(eprod_ok, 2 * u + 2)
                dve.tensor_reduce(e_dot[:, :], e_prod[:, :, :], AX.X, ALU.add).then_inc(edot_ok, 1)
                dve.wait_ge(edot_ok, u + 1)
                dve.tensor_tensor(logit[:, ds(u * TE, TE)], e_dot[:, 0:TE], e_dot[:, TE:GE],
                                  ALU.add).then_inc(logit_ok, 1)

            def p1(i):
                means(i, 0)
                centre(i, 0)
                means(i, 1)
                variances(2 * i, 0)
                centre(i, 1)
                if known(i, 1):
                    finish_nodes(2 * i - 2, 0)
                variances(2 * i + 1, 1)
                dve.wait_ge(evar_ok, 2 * i + 2)
                dve.wait_ge(nvar_ok, 2 * i + 2)
                dve.tensor_scalar(var_eps[:, :, :], var[:, :, :], LN_EPS, None, ALU.add).then_inc(vareps_ok, 1)
                if known(i, 1):
                    finish_nodes(2 * i - 1, 1)
                dve.wait_ge(std_ok, i + 1)
                dve.reciprocal(rstd[:, :, :], std[:, :, :]).then_inc(rstd_ok, 1)
                dve.wait_ge(rstd_ok, i + 1)
                if known(i, 1):
                    dve.wait_ge(resn_ok, 2 * i)
                normalise(i, 0)
                normalise(i, 1)

            def finish_nodes(u, s):
                dve.wait_ge(g2_ok, 2 * u + 2)
                dve.wait_ge(s1n_ok, u + 1)
                dve.tensor_tensor(resn[s][:, :, :], resn[s][:, :, :], s1n[s][:, :, :], ALU.add).then_inc(resn_ok, 1)

            p1(0)
            with dve.Fori(1, TRIPS - 1) as i:
                p1(i)
            p1(TRIPS - 1)
            finish_nodes(UNITS - 2, 0)
            finish_nodes(UNITS - 1, 1)

            mark = [0]

            def then_m(ins):
                mark[0] += 1
                ins.then_inc(m_step, 1)
                dve.wait_ge(m_step, mark[0])

            def by_row(bank):
                return psum[bank][0:RR, 0:RB * P].rearrange("r (b p) -> r b p", p=P)

            dve.wait_ge(m_pe, 1)
            then_m(dve.tensor_copy(z_row[:, :, :], by_row(0)))
            then_m(dve.scalar_tensor_tensor(out=e_row[:, :, :], in0=z_row[:, :, :], scalar=SLOPE,
                                            in1=z_row[:, :, :], op0=ALU.mult, op1=ALU.max))
            for b in range(RB):
                then_m(dve.tensor_tensor_scan(m_row[:, b, :], pen[:, b, :], e_row[:, b, :], -BIG, ALU.add, ALU.max))
            assert mark[0] == ROW_MAX_READY
            dve.wait_ge(m_pe, 2)
            then_m(dve.tensor_copy(line[0:1, :], psum[1][0:1, 0:2 * ET]))
            then_m(dve.tensor_tensor_scan(line_m[0:1, 1:ET + 1], line[0:1, ET:2 * ET], line[0:1, 0:ET], -BIG,
                                          ALU.add, ALU.max))
            assert mark[0] == LINE_READY
            dve.wait_ge(m_pe, 3)
            then_m(dve.tensor_copy(m_run[:, :, 0], psum[2][0:RR, 0:RB]))
            for b in range(RB):
                then_m(dve.tensor_tensor_scan(m_run[:, b, 1:P + 1], pen[:, b, :], e_row[:, b, :], m_run[:, b, 0:1],
                                              ALU.add, ALU.max))
            then_m(dve.tensor_tensor(d_row[:, :, :], m_run[:, :, 0:P], m_run[:, :, 1:P + 1], ALU.subtract))
            then_m(dve.tensor_scalar(d_row[:, :, :], d_row[:, :, :], 0.0, None, ALU.min))
            then_m(dve.tensor_tensor(z_row[:, :, :], e_row[:, :, :], m_run[:, :, 1:P + 1], ALU.subtract))
            assert mark[0] == DIFF_READY
            dve.wait_ge(m_act, 1)
            then_m(dve.tensor_tensor(decay_row[:, :, :], decay_row[:, :, :], same_prev[:, :, :], ALU.mult))
            assert mark[0] == DECAY_READY
            dve.wait_ge(m_pe, 4)
            then_m(dve.tensor_copy(weight[:, :], psum[3][0:P, 0:ET]))
            assert mark[0] == SM_DONE

            dve.wait_ge(p1_done, 1)
            dve.memset(acc[1][:, UE - 1:UE], 0.0).then_inc(p2_ready, 1)
            dve.memset(c1e[HC:HC + 1, :], 1.0).then_inc(p2_ready, 1)
            dve.wait_ge(p2_ready, 2)

            def weigh(i):
                if known(i, 1):
                    dve.wait_ge(wht_ps, 2 * i)
                t = ds(i * 2 * TE, 2 * TE)
                dve.tensor_tensor(wh[:, :, 0:D], keep[:, t, 0:D], bcast(weight[:, t], [P, 2 * TE, D], 2),
                                  ALU.mult).then_inc(wh_ok, 1)
                dve.tensor_copy(wh[:, :, D], weight[:, t]).then_inc(whw_ok, 1)

            weigh(0)

            def p2(i):
                t = ds(i * 2 * TE, 2 * TE)
                dve.tensor_tensor(x_last[:, :, :], keep[:, t, D:2 * D], bcast(last_f[:, t], [P, 2 * TE, D], 2),
                                  ALU.mult).then_inc(xlast_ok, 1)
                for s in range(2):
                    u = 2 * i + s
                    dve.wait_ge(wht_ps, u + 1)
                    dve.wait_ge(d_dec[s], 16 * (i + 1))
                    if known(u, 1):
                        dve.wait_ge(acc_ok, u)
                    if known(u, 2):
                        dve.wait_ge(num_ps, u - 1)
                    dve.tensor_tensor_scan(acc[s][:, :], decay[s][:, :], psum[s][0:D1, 0:UE],
                                           acc[1 - s][:, UE - 1:UE], ALU.mult, ALU.add).then_inc(acc_ok, 1)
                dve.wait_ge(num_ps, 2 * i + 2)
                num = psum_all[0:P, 2:4, 0:TE * D1].rearrange("p b (j d) -> p b j d", d=D1)
                dve.tensor_scalar(den_eps[:, :].rearrange("p (b j) -> p b j", b=2), num[:, :, :, D], SM_EPS, None,
                                  ALU.add).then_inc(dene_ok, 1)
                dve.wait_ge(dene_ok, i + 1)
                dve.reciprocal(den_inv[:, :], den_eps[:, :]).then_inc(deni_ok, 1)
                dve.wait_ge(deni_ok, i + 1)
                dve.tensor_tensor(den_last[:, :], den_inv[:, :], last_f[:, t], ALU.mult).then_inc(denl_ok, 1)
                dve.wait_ge(denl_ok, i + 1)
                for s in range(2):
                    ins = dve.tensor_tensor(att_out[:, s * TE:(s + 1) * TE, :], num[:, s, :, 0:D],
                                            bcast(den_last[:, s * TE:(s + 1) * TE], [P, TE, D], 2), ALU.mult)
                ins.then_inc(att_ok, 1)
                if not (isinstance(i, int) and i == TRIPS - 1):
                    weigh(i + 1)
                dve.wait_ge(th_ok, i + 1)
                dve.wait_ge(xlast_ok, i + 1)
                if known(i, 1):
                    dve.wait_ge(x1k_ok, i)
                dve.tensor_tensor(x1_last[:, :, :], x_last[:, :, :], att_th[:, :, :], ALU.add).then_inc(x1_ok, 1)
                dve.wait_ge(x1_ok, i + 1)
                dve.tensor_reduce(l_sum[:, :], x1_last[:, :, :], AX.X, ALU.add).then_inc(lsum_ok, 1)
                dve.wait_ge(lsum_ok, i + 1)
                dve.tensor_scalar(l_mean[:, :], l_sum[:, :], 1.0 / D, None, ALU.mult).then_inc(lmean_ok, 1)
                dve.wait_ge(lmean_ok, i + 1)
                dve.tensor_tensor(l_cen[:, :, :], x1_last[:, :, :], bcast(l_mean[:, :], [P, 2 * TE, D], 2),
                                  ALU.subtract).then_inc(lcen_ok, 1)
                for s in range(2):
                    if known(i, 1):
                        dve.wait_ge(d_sc[s], 16 * TE * i)
                    dve.tensor_copy(lidx[s][:, :], last_idx[:, ds(2 * i * TE + s * TE, TE)]).then_inc(lidx_ok, 1)
                dve.wait_ge(lsq_ok, i + 1)
                dve.tensor_reduce(l_var[:, :], l_sq[:, :, :], AX.X, ALU.add).then_inc(lvar_ok, 1)
                dve.wait_ge(lvar_ok, i + 1)
                dve.tensor_scalar(l_eps[:, :], l_var[:, :], LN_EPS, None, ALU.add).then_inc(leps_ok, 1)
                dve.wait_ge(lstd_ok, i + 1)
                dve.reciprocal(l_rstd[:, :], l_std[:, :]).then_inc(lrstd_ok, 1)
                dve.wait_ge(lrstd_ok, i + 1)
                for s in range(2):
                    if known(i, 1):
                        dve.wait_ge(h1k_ok, 2 * i - 1 + s)
                    dve.scalar_tensor_tensor(out=h1e[s][:, :, :], in0=l_cen[:, s * TE:(s + 1) * TE, :], scalar=0.0,
                                             in1=bcast(l_rstd[:, s * TE:(s + 1) * TE], [P, TE, D], 2),
                                             op0=ALU.max, op1=ALU.mult).then_inc(h1e_ok, 1)

            p2(0)
            with dve.Fori(1, TRIPS - 1) as i:
                p2(i)
            p2(TRIPS - 1)

            def stage_src(i, s):
                v = 2 * i + s
                if known(v, 2):
                    dve.wait_ge(d_cat[s], 16 * TE * i)
                dve.tensor_copy(sidx[s][:, :],
                                gather_idx[:, ds(mirror(i, s), 1), 0:TE].rearrange("p a g -> p (a g)"))\
                    .then_inc(sidx_ok, 1)

            def stage_first(i, s):
                v = 2 * i + s
                if known(v, 2):
                    dve.wait_ge(d_fin[s], 16 * TE * i)
                dve.tensor_copy(fidx[s][:, :], first_idx[:, ds(mirror(i, s) * TE, TE)]).then_inc(fidx_ok, 1)

            def box_sums(v, s):
                dve.wait_ge(m2_ok, v + 1)
                if known(v, 1):
                    dve.wait_ge(box_ok, v)
                if known(v, 2):
                    dve.wait_ge(ce_ps, v - 1)
                dve.tensor_tensor_scan(box[s][:, ::-1], same[s][0:D, ::-1], msg[:, ::-1],
                                       box[1 - s][:, 0:1], ALU.mult, ALU.add).then_inc(box_ok, 1)

            def finish_edges(i, s):
                v = 2 * i + s
                dve.wait_ge(ge_ok, v + 1)
                stage_first(i, s)
                dve.tensor_tensor(res[s][:, :, :], g3[:, :, :],
                                  psum[6][0:P, 256:512].rearrange("p (j d) -> p j d", d=D), ALU.add)\
                    .then_inc(res_ok, 1)

            dve.memset(fill[1][:, 0:1], 0.0).then_inc(p2_ready, 1)
            dve.memset(box[1][:, 0:1], 0.0).then_inc(p2_ready, 1)
            dve.wait_ge(p2_ready, 4)
            stage_src(0, 0)
            stage_src(0, 1)

            def p3(i):
                for s in range(2):
                    v = 2 * i + s
                    if known(v, 1):
                        box_sums(v - 1, 1 - s)
                    dve.wait_ge(keptt_ps, v + 1)
                    dve.wait_ge(d_same[s], 16 * (i + 1))
                    if known(v, 1):
                        dve.wait_ge(fill_ok, v)
                    if known(v, 2):
                        dve.wait_ge(ge_ps, v - 1)
                    dve.tensor_tensor_scan(fill[s][:, ::-1], same[s][:, ::-1], psum[s][:, UE - 1::-1],
                                           fill[1 - s][:, 0:1], ALU.mult, ALU.add).then_inc(fill_ok, 1)
                    if not (isinstance(i, int) and i == TRIPS - 1):
                        stage_src(i + 1, s)
                    if known(v, 1):
                        finish_edges(i - 1 + s, 1 - s)

            p3(0)
            with dve.Fori(1, TRIPS - 1) as i:
                p3(i)
            p3(TRIPS - 1)
            box_sums(UNITS - 1, 1)
            finish_edges(TRIPS - 1, 1)

        @block.tensor
        def _(pe):
            pe.wait_ge(ident_ok, 1)
            pe.wait_ge(c_step, ROWS_READY)
            for b in range(RB):
                pe.transpose(psum[0][0:P, b * RR:(b + 1) * RR], row_src_f[:, b, :], ident[0:RR, 0:RR])
                pe.transpose(psum[0][0:P, 256 + b * RR:256 + (b + 1) * RR], row_dst_f[:, b, 1:P + 1], ident[0:RR, 0:RR])
                pe.transpose(psum[1][0:P, b * RR:(b + 1) * RR], same_prev[:, b, :], ident[0:RR, 0:RR])
                last = pe.transpose(psum[1][0:P, 256 + b * RR:256 + (b + 1) * RR], same_next[:, b, :], ident[0:RR, 0:RR])
            last.then_inc(c_pe, 1)
            pe.wait_ge(d_w, 16 * 17)
            pe.transpose(psum[2][0:D, 0:D], w0_ext[0:D, 0:D], ident[0:D, 0:D]).then_inc(c_pe, 1)
            pe.wait_ge(c_step, ATT_READY)
            for g in range(2):
                last = pe.matmul(psum[2][:, 64 + g * D:64 + (g + 1) * D], att_rep[:, g, :], w0_t[:, :],
                                 start=True, stop=True)
            last.then_inc(c_pe, 1)

            def out_layer(u, s):
                for h in range(2):
                    pe.wait_ge(c1_ok, 4 * u + 2 * h + 2)
                    if known(u, 1):
                        pe.wait_ge(g2_ok, 2 * u - 1 + h)
                    for j in range(TN // 2):
                        t = 8 * h + j
                        q, c = t % 2, t // 2
                        last = pe.matmul(psum[6 + h][0:P, j * D:(j + 1) * D],
                                         c1t[:, 2 * (c // 4) + q, (c % 4) * P:(c % 4 + 1) * P],
                                         wc2_ext[:, :], start=True, stop=True)
                    last.then_inc(z2_ps, 1)

            def turn(u, s):
                pe.wait_ge(h1n_ok, u + 1)
                if known(u, 1):
                    pe.wait_ge(h1t_ok, 2 * u)
                for c in range(TN // 2):
                    last = pe.transpose(psum[c // 4][:, (c % 4) * P:(c % 4 + 1) * P],
                                        h1n[s][:, 2 * c:2 * c + 2, :].rearrange("p j d -> p (j d)"),
                                        ident[0:P, 0:P])
                last.then_inc(h1t_ps, 1)

            def hidden_layer(u, s):
                for k in range(2):
                    pe.wait_ge(h1t_ok, 2 * u + k + 1)
                    for q in range(2):
                        if known(u, 1):
                            pe.wait_ge(c1_ok, 4 * u - 3 + 2 * k + q)
                        pe.matmul(psum[2 + 2 * k + q][0:HC, 0:4 * P], wc1_top[q * D:(q + 1) * D, :],
                                  h1t[q * D:(q + 1) * D, k, :], start=True, stop=True).then_inc(c1_ps, 1)

            def p1(i):
                turn(2 * i, 0)
                hidden_layer(2 * i, 0)
                turn(2 * i + 1, 1)
                out_layer(2 * i, 0)
                hidden_layer(2 * i + 1, 1)
                out_layer(2 * i + 1, 1)

            pe.wait_ge(c_step, CONST_READY)
            trips(pe, p1)

            pe.wait_ge(logit_ok, UNITS)
            pe.wait_ge(h1t_ok, 2 * UNITS)
            pe.wait_ge(c1_ok, 4 * UNITS)
            for b in range(RB):
                last = pe.transpose(psum[0][0:RR, b * P:(b + 1) * P], logit[:, b * RR:(b + 1) * RR], ident[0:P, 0:P])
            last.then_inc(m_pe, 1)
            pe.wait_ge(m_step, ROW_MAX_READY)
            for b in range(RB):
                pe.transpose(psum[1][0:1, b * RR:(b + 1) * RR], m_row[:, b, P - 1:P], ident[0:RR, 0:RR])
                last = pe.transpose(psum[1][0:1, ET + b * RR:ET + (b + 1) * RR], pen_min[:, b:b + 1],
                                    ident[0:RR, 0:RR])
            last.then_inc(m_pe, 1)
            pe.wait_ge(m_step, LINE_READY)
            for b in range(RB):
                last = pe.transpose(psum[2][0:RR, b:b + 1], line_m[0:1, b * RR:(b + 1) * RR], ident[0:1, 0:1])
            last.then_inc(m_pe, 1)
            pe.wait_ge(m_act, 2)
            for b in range(RB):
                last = pe.transpose(psum[3][0:P, b * RR:(b + 1) * RR], w_row[:, b, :], ident[0:RR, 0:RR])
            last.then_inc(m_pe, 1)

            pe.wait_ge(p1_done, 1)

            def p2(i):
                for s in range(2):
                    u = 2 * i + s
                    if s == 0:
                        pe.wait_ge(wh_ok, i + 1)
                        pe.wait_ge(whw_ok, i + 1)
                    if known(u, 2):
                        pe.wait_ge(acc_ok, u - 1)
                    for j in range(TE):
                        last = pe.transpose(psum[s][0:D1, j * P:(j + 1) * P], wh[:, s * TE + j, :], ident[0:P, 0:P])
                    last.then_inc(wht_ps, 1)
                for s in range(2):
                    u = 2 * i + s
                    pe.wait_ge(acc_ok, u + 1)
                    if s == 0 and known(i, 1):
                        pe.wait_ge(att_ok, i)
                    for j in range(TE):
                        last = pe.matmul(psum[2 + s][0:P, j * D1:(j + 1) * D1], acc[s][:, j * P:(j + 1) * P],
                                         w0_ext[:, :], start=True, stop=True)
                    last.then_inc(num_ps, 1)

            trips(pe, p2)

            def turn_edges(v, s, i):
                pe.wait_ge(kept_ok, v + 1)
                if known(v, 2):
                    pe.wait_ge(fill_ok, v - 1)
                for j in range(TE):
                    last = pe.transpose(psum[s][:, j * P:(j + 1) * P], kept[s][:, j, :], ident[0:P, 0:P])
                last.then_inc(keptt_ps, 1)
                pe.wait_ge(d_cat[s], 16 * TE * (i + 1))
                pe.wait_ge(d_ea[s], 16 * (i + 1))
                if known(v, 1):
                    pe.wait_ge(catt_ok, v)
                for j in range(TE):
                    last = pe.transpose(psum[2][0:D + DE, j * P:(j + 1) * P], cat[s][:, j, :], ident[0:P, 0:P])
                last.then_inc(catt_ps, 1)

            def node_hidden(v, s):
                pe.wait_ge(box_ok, v + 1)
                if known(v, 1):
                    pe.wait_ge(ce_ok, v)
                pe.matmul(psum[5][0:HC, 0:UE], wc1_top[0:D, :], fill[s][0:D, :], start=True, stop=False)
                pe.matmul(psum[5][0:HC, 0:UE], wc1_box[:, :], box[s][:, :], start=False, stop=True).then_inc(ce_ps, 1)

            def node_out(v, s):
                pe.wait_ge(ce_ok, v + 1)
                if known(v, 1):
                    pe.wait_ge(res_ok, v)
                for j in range(TE):
                    pe.matmul(psum[6][0:P, j * D:(j + 1) * D], c1e[:, j * P:(j + 1) * P], wc2_ext[:, :],
                              start=True, stop=True)
                for j in range(TE):
                    last = pe.matmul(psum[6][0:P, 256 + j * D:256 + (j + 1) * D], fill[s][:, j * P:(j + 1) * P],
                                     stack_id[:, :], start=True, stop=True)
                last.then_inc(ge_ps, 1)

            def p3(i):
                for s in range(2):
                    v = 2 * i + s
                    turn_edges(v, s, i)
                    if known(v, 1):
                        node_hidden(v - 1, 1 - s)
                    pe.wait_ge(catt_ok, v + 1)
                    pe.wait_ge(fill_ok, v + 1)
                    if known(v, 1):
                        pe.wait_ge(m1_ok, v)
                    pe.matmul(psum[3][0:HM, 0:UE], wm1_src[:, :], cat_t[:, :], start=True, stop=False)
                    pe.matmul(psum[3][0:HM, 0:UE], wm1_dst[:, :], fill[s][0:D, :], start=False, stop=True)\
                        .then_inc(m1_ps, 1)
                    if known(v, 1):
                        node_out(v - 1, 1 - s)
                    pe.wait_ge(m1_ok, v + 1)
                    if known(v, 1):
                        pe.wait_ge(m2_ok, v)
                    pe.matmul(psum[4][0:D, 0:UE], wm2[:, :], msg_h[:, :], start=True, stop=True).then_inc(m2_ps, 1)

            trips(pe, p3)
            node_hidden(UNITS - 1, 1)
            node_out(UNITS - 1, 1)


ROWS_READY = 8
ATT_READY = 24
CONST_READY = 26
ROW_MAX_READY = 4
LINE_READY = 6
DIFF_READY = 12
DECAY_READY = 13
SM_DONE = 14

_INS = ['x', 'src', 'dst', 'edge_attr_32', 'L0_gnn_W', 'L0_gnn_att_src', 'L0_gnn_att_dst', 'L0_gnn_bias',
        'L1_gnn_W_m1', 'L1_gnn_b_m1', 'L1_gnn_W_m2', 'L1_gnn_b_m2', 'L1_gnn_W_c1', 'L1_gnn_b_c1', 'L1_gnn_W_c2',
        'L1_gnn_b_c2']
_OUTS = [((100000, 64), 'float32')]


def kernel(**inputs):
    import numpy as _np
    import concourse.bacc as _bacc
    from concourse import mybir as _mybir
    from concourse.bass_utils import run_bass_kernel_spmd as _run

    nc = _bacc.Bacc("TRN2", target_bir_lowering=False, num_devices=1)
    arrays, args = {}, []
    for name in _INS:
        a = _np.ascontiguousarray(inputs[name])
        arrays[f"in_{name}_dram"] = a
        args.append(nc.dram_tensor(f"in_{name}_dram", a.shape, _mybir.dt.from_np(a.dtype), kind="ExternalInput").ap())
    for i, (shape, dtype) in enumerate(_OUTS):
        dt = _mybir.dt.from_np(_np.dtype(dtype))
        args.append(nc.dram_tensor(f"out_{i}_dram", shape, dt, kind="ExternalOutput").ap())
    gnn_two_layer_kernel(nc, *args)
    r = _run(nc, [arrays], core_ids=[0])
    return r.results[0]["out_0_dram"]
```

```python
import concourse.bass as bass
from concourse import mybir
from contextlib import ExitStack


def gnn_two_layer_kernel(
    nc: bass.Bass,
    x: bass.AP,
    src: bass.AP,
    dst: bass.AP,
    edge_attr: bass.AP,
    W0: bass.AP,
    att_src: bass.AP,
    att_dst: bass.AP,
    bias0: bass.AP,
    W_m1: bass.AP,
    b_m1: bass.AP,
    W_m2: bass.AP,
    b_m2: bass.AP,
    W_c1: bass.AP,
    b_c1: bass.AP,
    W_c2: bass.AP,
    b_c2: bass.AP,
    out: bass.AP,
):
    fp32 = mybir.dt.float32
    i32 = mybir.dt.int32
    ALU = mybir.AluOpType
    ACT = mybir.ActivationFunctionType
    AX = mybir.AxisListType
    ds = bass.ds

    N, D = x.shape
    E = src.shape[0]
    DE = edge_attr.shape[1]
    HM = W_m1.shape[1]
    HC = W_c1.shape[1]
    P = 125
    ET = E // P
    TE = 4
    UNITS = ET // TE
    UE = TE * P
    TN = N // UNITS // P
    UN = TN * P
    GE = 2 * TE
    RB = 2
    RR = ET // RB
    PM = 120
    LN_EPS = 1e-5
    SM_EPS = 1e-16
    SLOPE = 0.2
    BIG = 1.0e30
    SKIP = float(1 << 20)
    D1 = D + 1
    TRIPS = UNITS // 2
    assert E == ET * P and ET == UNITS * TE and N == UNITS * UN and UNITS % 2 == 0

    node_table = nc.dram_tensor("node_table", [N, D], fp32).ap()
    decay_dram = nc.dram_tensor("decay_dram", [E], fp32).ap()
    same_dram = nc.dram_tensor("same_dram", [E], fp32).ap()

    def known(u, least):
        return not isinstance(u, int) or u >= least

    def mirror(i, s):
        return i * -2 + (UNITS - 1 - s)

    def bcast(ap, shape, axis):
        return ap.unsqueeze(axis).broadcast_to(shape)

    def rows_of(dram):
        return dram.rearrange("(b r p) -> r b p", b=RB, p=P)

    ctx = ExitStack()
    first_phase = ExitStack()
    with ctx:
        scope = [ctx]

        def sb(name, shape, dt=fp32):
            return scope[0].enter_context(nc.sbuf_tensor(name, shape, dt))

        def sem(name):
            return ctx.enter_context(nc.semaphore(name))

        def two(name, shape, dt=fp32):
            return [sb(f"{name}{s}", shape, dt) for s in range(2)]

        ident = sb("ident", [128, 128])
        stack_id = sb("stack_id", [128, D])
        w0_ext = sb("w0_ext", [D1, D1])
        w0_t = sb("w0_t", [D, D])
        att_col = sb("att_col", [D, 2])
        att_rep = sb("att_rep", [D, 2, 128])
        att_vec = sb("att_vec", [P, GE, D])
        tanh_b = sb("tanh_b", [P, D])
        wc1_top = sb("wc1_top", [128, HC])
        wc1_box = sb("wc1_box", [D, HC])
        wc2_ext = sb("wc2_ext", [HC + 1, D])
        wm1_dst = sb("wm1_dst", [D, HM])
        wm1_src = sb("wm1_src", [D + DE, HM])
        wm2 = sb("wm2", [HM, D])
        bc1 = sb("bc1", [HC, 1])
        bc2 = sb("bc2", [2 * D, 1])
        bm1 = sb("bm1", [HM, 1])
        bm2 = sb("bm2", [D, 1])
        row_dst = sb("row_dst", [RR, RB, P + 2], i32)
        row_src = sb("row_src", [RR, RB, P], i32)
        row_dst_f = sb("row_dst_f", [RR, RB, P + 2])
        row_src_f = sb("row_src_f", [RR, RB, P])
        same_prev = sb("same_prev", [RR, RB, P])
        same_next = sb("same_next", [RR, RB, P])
        gather_idx = sb("gather_idx", [P, UNITS, GE], i32)
        dst_f = sb("dst_f", [P, ET])
        last_f = sb("last_f", [P, ET])
        first_f = sb("first_f", [P, ET])
        tmp_l = sb("tmp_l", [P, ET])
        tmp_f = sb("tmp_f", [P, ET])
        last_idx = sb("last_idx", [P, ET], i32)
        first_idx = sb("first_idx", [P, ET], i32)
        keep = sb("keep", [P, ET, 2 * D])
        logit = sb("logit", [P, ET])
        weight = sb("weight", [P, ET])
        scope[0] = first_phase
        idx_now = two("idx_now", [P, GE], i32)
        xe = two("xe", [P, GE, D])
        e_sum = two("e_sum", [P, GE])
        e_cen = two("e_cen", [P, GE, D])
        e_sq = sb("e_sq", [P, GE, D])
        e_prod = sb("e_prod", [P, GE, D])
        e_sc = sb("e_sc", [P, GE])
        e_dot = two("e_dot", [P, GE])
        xn = two("xn", [P, TN, D])
        x1n = two("x1n", [P, TN, D])
        n_sum = two("n_sum", [P, TN])
        n_sq = sb("n_sq", [P, TN, D])
        h1n = two("h1n", [P, TN, D])
        s1n = two("s1n", [P, TN, D])
        h1t = sb("h1t", [128, 2, 4 * P])
        c1t = sb("c1t", [HC, 4, 4 * P])
        g2t = sb("g2t", [2 * D, 2, 4 * P])
        resn = two("resn", [P, TN, D])
        var = sb("var", [P, 2, TN + GE])
        ln_eps = sb("ln_eps", [P, 1])
        std = sb("std", [P, 2, TN + GE])
        rstd = sb("rstd", [P, 2, TN + GE])
        pen = sb("pen", [RR, RB, P])
        pen_min = sb("pen_min", [RR, RB])
        z_row = sb("z_row", [RR, RB, P])
        e_row = sb("e_row", [RR, RB, P])
        m_row = sb("m_row", [RR, RB, P])
        m_run = sb("m_run", [RR, RB, P + 1])
        line = sb("line", [1, 2 * ET])
        line_m = sb("line_m", [1, ET + 1])
        d_row = sb("d_row", [RR, RB, P])
        decay_row = sb("decay_row", [RR, RB, P])
        w_row = sb("w_row", [RR, RB, P])
        first_phase.close()
        scope[0] = ctx
        wh = sb("wh", [P, 2 * TE, D1])
        decay = two("decay", [D1, UE])
        acc = two("acc", [D1, UE])
        lidx = two("lidx", [P, TE], i32)
        x_last = sb("x_last", [P, 2 * TE, D])
        den_eps = sb("den_eps", [P, 2 * TE])
        den_inv = sb("den_inv", [P, 2 * TE])
        den_last = sb("den_last", [P, 2 * TE])
        att_out = sb("att_out", [P, 2 * TE, D])
        x1_last = sb("x1_last", [P, 2 * TE, D])
        att_th = sb("att_th", [P, 2 * TE, D])
        l_sum = sb("l_sum", [P, 2 * TE])
        l_mean = sb("l_mean", [P, 2 * TE])
        l_cen = sb("l_cen", [P, 2 * TE, D])
        l_sq = sb("l_sq", [P, 2 * TE, D])
        l_var = sb("l_var", [P, 2 * TE])
        l_eps = sb("l_eps", [P, 2 * TE])
        l_std = sb("l_std", [P, 2 * TE])
        l_rstd = sb("l_rstd", [P, 2 * TE])
        h1e = two("h1e", [P, TE, D])
        sidx = two("sidx", [P, TE], i32)
        fidx = two("fidx", [P, TE], i32)
        cat = two("cat", [P, TE, D + DE])
        kept = two("kept", [P, TE, 2 * D])
        cat_t = sb("cat_t", [D + DE, UE])
        same = two("same", [128, UE])
        fill = two("fill", [128, UE])
        msg_h = sb("msg_h", [HM, UE])
        msg = sb("msg", [D, UE])
        box = two("box", [D, UE])
        c1e = sb("c1e", [HC + 1, UE])
        g3 = sb("g3", [P, TE, D])
        res = two("res", [P, TE, D])

        psum_all = ctx.enter_context(nc.psum_tensor("psum_all", [128, 8, 512], fp32))
        psum = [psum_all[:, i, :] for i in range(8)]

        d_pad = sem("d_pad")
        sp_turn = sem("sp_turn")
        pool_turn = sem("pool_turn")
        d_rows = sem("d_rows")
        d_w = sem("d_w")
        ident_z = sem("ident_z")
        ident_ok = sem("ident_ok")
        c_step = sem("c_step")
        c_pe = sem("c_pe")
        c_act = sem("c_act")
        nx_out = sem("nx_out")
        tables = sem("tables")
        idx_ok = sem("idx_ok")
        d_xe = [sem(f"d_xe{s}") for s in range(2)]
        esum_ok = sem("esum_ok")
        ecen_ok = sem("ecen_ok")
        esq_ok = sem("esq_ok")
        evar_ok = sem("evar_ok")
        std_ok = sem("std_ok")
        rstd_ok = sem("rstd_ok")
        eprod_ok = sem("eprod_ok")
        edot_ok = sem("edot_ok")
        esc_ok = sem("esc_ok")
        keeph_ok = sem("keeph_ok")
        logit_ok = sem("logit_ok")
        xdst_ok = sem("xdst_ok")
        d_xn = [sem(f"d_xn{s}") for s in range(2)]
        nx1_ok = [sem(f"nx1_ok{s}") for s in range(2)]
        nsum_ok = sem("nsum_ok")
        ncen_ok = sem("ncen_ok")
        nsq_ok = sem("nsq_ok")
        nvar_ok = sem("nvar_ok")
        h1n_ok = sem("h1n_ok")
        s1n_ok = [sem(f"s1n_ok{s}") for s in range(2)]
        h1t_ps = sem("h1t_ps")
        h1t_ok = sem("h1t_ok")
        c1_ps = sem("c1_ps")
        c1_ok = sem("c1_ok")
        z2_ps = sem("z2_ps")
        g2_ok = sem("g2_ok")
        g2_ps = sem("g2_ps")
        resn_ok = sem("resn_ok")
        d_tab = [sem(f"d_tab{s}") for s in range(2)]
        d_res = [sem(f"d_res{s}") for s in range(2)]
        m_step = sem("m_step")
        m_pe = sem("m_pe")
        m_act = sem("m_act")
        d_flow = sem("d_flow")

        p1_done = sem("p1_done")
        p2_ready = sem("p2_ready")
        wh_ok = sem("wh_ok")
        whw_ok = sem("whw_ok")
        wht_ps = sem("wht_ps")
        d_dec = [sem(f"d_dec{s}") for s in range(2)]
        acc_ok = sem("acc_ok")
        num_ps = sem("num_ps")
        xlast_ok = sem("xlast_ok")
        dene_ok = sem("dene_ok")
        deni_ok = sem("deni_ok")
        denl_ok = sem("denl_ok")
        att_ok = sem("att_ok")
        th_ok = sem("th_ok")
        x1_ok = sem("x1_ok")
        x1k_ok = sem("x1k_ok")
        lsum_ok = sem("lsum_ok")
        lmean_ok = sem("lmean_ok")
        lcen_ok = sem("lcen_ok")
        lsq_ok = sem("lsq_ok")
        lvar_ok = sem("lvar_ok")
        leps_ok = sem("leps_ok")
        lstd_ok = sem("lstd_ok")
        lrstd_ok = sem("lrstd_ok")
        h1e_ok = sem("h1e_ok")
        h1k_ok = sem("h1k_ok")
        lidx_ok = sem("lidx_ok")
        d_sc = [sem(f"d_sc{s}") for s in range(2)]
        p2_done = sem("p2_done")
        sidx_ok = sem("sidx_ok")
        fidx_ok = sem("fidx_ok")
        d_cat = [sem(f"d_cat{s}") for s in range(2)]
        d_ea = [sem(f"d_ea{s}") for s in range(2)]
        d_same = [sem(f"d_same{s}") for s in range(2)]
        kept_ok = sem("kept_ok")
        catt_ps = sem("catt_ps")
        catt_ok = sem("catt_ok")
        keptt_ps = sem("keptt_ps")
        fill_ok = sem("fill_ok")
        m1_ps = sem("m1_ps")
        m1_ok = sem("m1_ok")
        m2_ps = sem("m2_ps")
        m2_ok = sem("m2_ok")
        box_ok = sem("box_ok")
        ce_ps = sem("ce_ps")
        ce_ok = sem("ce_ok")
        ge_ps = sem("ge_ps")
        ge_ok = sem("ge_ok")
        res_ok = sem("res_ok")
        d_fin = [sem(f"d_fin{s}") for s in range(2)]

        block = ctx.enter_context(nc.Block())

        def trips(eng, trip):
            trip(0)
            with eng.Fori(1, TRIPS) as i:
                trip(i)

        @block.sync
        def _(sp):
            with nc.allow_non_contiguous_dma(reason="one neighbour per row of 125 destinations"):
                sp.wait_ge(d_pad, 1)
                sp.dma_start(row_dst[:, :, 1:P + 1], rows_of(dst)).then_inc(d_rows, 16)
                sp.dma_start(row_src[:, :, :], rows_of(src)).then_inc(d_rows, 16)
                before = dst[P - 1:E].rearrange("(t o) -> t o", o=1)
                after = dst[P:E].rearrange("(t o) -> t o", o=1)
                for b in range(RB):
                    lo = 1 if b == 0 else 0
                    hi = RR if b < RB - 1 else RR - 1
                    t0 = b * RR + lo - 1
                    sp.dma_start(row_dst[lo:RR, b, 0:1],
                                 before[P * t0:P * (t0 + RR - lo - 1) + 1:P, :]).then_inc(d_rows, 16)
                    sp.dma_start(row_dst[0:hi, b, P + 1:P + 2],
                                 after[P * b * RR:P * (b * RR + hi - 1) + 1:P, :]).then_inc(d_rows, 16)
            for to, frm in (
                (w0_ext[0:D, 0:D], W0), (w0_ext[D:D1, 0:D], bias0.unsqueeze(0)),
                (att_col[:, 0:1], att_src.unsqueeze(1)), (att_col[:, 1:2], att_dst.unsqueeze(1)),
                (tanh_b[:, :], bias0.partition_broadcast(P)),
                (wc1_top[0:D, :], W_c1[0:D, :]), (wc1_top[D:2 * D, :], W_c1[0:D, :]),
                (wc1_box[:, :], W_c1[D:2 * D, :]),
                (wc2_ext[0:HC, :], W_c2), (wc2_ext[HC:HC + 1, :], b_c2.unsqueeze(0)),
                (wm1_src[0:D, :], W_m1[0:D, :]), (wm1_dst[:, :], W_m1[D:2 * D, :]),
                (wm1_src[D:D + DE, :], W_m1[2 * D:2 * D + DE, :]), (wm2[:, :], W_m2),
                (bc1[:, :], b_c1.unsqueeze(1)), (bm1[:, :], b_m1.unsqueeze(1)),
                (bc2[0:D, :], b_c2.unsqueeze(1)), (bc2[D:2 * D, :], b_c2.unsqueeze(1)), (bm2[:, :], b_m2.unsqueeze(1)),
            ):
                sp.dma_start(to, frm).then_inc(d_w, 16)

            def nodes(dram, u):
                return dram[ds(u * UN, UN), :].rearrange("(p j) d -> p j d", j=TN)

            def load(u, s):
                for a, b in ((0, PM), (PM, P)):
                    sp.dma_start(xn[s][a:b, :, :], nodes(x, u)[a:b]).then_inc(d_xn[s], 16)

            load(0, 0)
            load(1, 1)

            def store_table(u, s):
                sp.wait_ge(h1n_ok, u + 1)
                for a, b in ((0, PM), (PM, P)):
                    sp.dma_start(nodes(node_table, u)[a:b], h1n[s][a:b, :, :]).then_inc(d_tab[s], 16)

            def store_result(u, s):
                sp.wait_ge(resn_ok, u + 1)
                for a, b in ((0, PM), (PM, P)):
                    sp.dma_start(nodes(out, u)[a:b], resn[s][a:b, :, :]).then_inc(d_res[s], 16)

            def p1(i):
                for s in range(2):
                    if not (isinstance(i, int) and i == TRIPS - 1):
                        sp.wait_ge(nx1_ok[s], i + 1)
                        load(2 * i + s + 2, s)
                if known(i, 1):
                    store_result(2 * i - 2, 0)
                for s in range(2):
                    store_table(2 * i + s, s)
                if known(i, 1):
                    store_result(2 * i - 1, 1)

            p1(0)
            with sp.Fori(1, TRIPS - 1) as i:
                p1(i)
            p1(TRIPS - 1)
            for s in range(2):
                store_result(UNITS - 2 + s, s)

            sp.dma_start(rows_of(same_dram), same_next[:, :, :]).then_inc(d_flow, 16)
            sp.wait_ge(m_step, DECAY_READY)
            sp.dma_start(rows_of(decay_dram), decay_row[:, :, :]).then_inc(d_flow, 16)
            sp.wait_ge(d_flow, 32)
            for s in range(2):
                sp.wait_ge(d_tab[s], 32 * TRIPS)
                sp.wait_ge(d_res[s], 32 * TRIPS)
            sp.wait_ge(m_step, SM_DONE)
            sp.sem_inc(p1_done)

            def load_decay(u, s):
                sp.dma_start(decay[s][:, :], decay_dram[ds(u * UE, UE)].partition_broadcast(D1)).then_inc(d_dec[s], 16)

            def p2(i):
                for s in range(2):
                    u = 2 * i + s
                    if known(u, 2):
                        sp.wait_ge(acc_ok, u - 1)
                        sp.sem_inc(sp_turn)
                    load_decay(u, s)

            trips(sp, p2)

            def load_edges(i, s):
                e0 = mirror(i, s) * UE
                sp.dma_start(same[s][:, :], same_dram[ds(e0, UE)].partition_broadcast(128)).then_inc(d_same[s], 16)
                sp.dma_start(cat[s][:, :, D:D + DE], edge_attr[ds(e0, UE), :].rearrange("(j p) d -> p j d", p=P))\
                    .then_inc(d_ea[s], 16)

            def p3(i):
                for s in range(2):
                    v = 2 * i + s
                    if known(v, 2):
                        sp.wait_ge(box_ok, v - 1)
                        sp.wait_ge(catt_ps, v - 1)
                        sp.sem_inc(sp_turn)
                    load_edges(i, s)

            trips(sp, p3)

        @block.gpsimd
        def _(pool):
            pool.memset(row_dst[:, :, :], -1).then_inc(d_pad, 1)
            pool.memset(ident[:, :], 0.0).then_inc(ident_z, 1)
            pool.wait_ge(ident_z, 1)
            pool.affine_select(out=ident[:, :], in_=ident[:, :], compare_op=ALU.not_equal, fill=1.0,
                               base=0, pattern=[[-1, 128]], channel_multiplier=1).then_inc(ident_ok, 1)

            last_node = pool.to_reg(N - 1)

            def p1(i):
                for s in range(2):
                    u = 2 * i + s
                    pool.wait_ge(idx_ok, u + 1)
                    if known(u, 2):
                        pool.wait_ge(ecen_ok, u - 1)
                        pool.wait_ge(xdst_ok, u - 1)
                    pool.sem_inc(pool_turn)
                    for g in range(GE):
                        pool.indirect_dma_start(
                            out=xe[s][:, g, :], out_offset=None, in_=x,
                            in_offset=bass.IndirectOffsetOnAxis(ap=idx_now[s][:, g:g + 1], axis=0),
                            bounds_check=last_node, oob_is_err=False).then_inc(d_xe[s], 16)


            def node_x1(i):
                pool.wait_ge(d_xn[1], 32 * (i + 1))
                if known(i, 1):
                    pool.wait_ge(s1n_ok[1], i)
                pool.tensor_tensor(x1n[1][:, :, :], xn[1][:, :, :], bcast(tanh_b[:, :], [P, TN, D], 1), ALU.add)\
                    .then_inc(nx1_ok[1], 1)

            def add_nodes(i):
                pool.wait_ge(h1n_ok, 2 * i + 2)
                if known(i, 1):
                    pool.wait_ge(resn_ok, 2 * i)
                pool.tensor_tensor(s1n[1][:, :, :], x1n[1][:, :, :], h1n[1][:, :, :], ALU.add).then_inc(s1n_ok[1], 1)

            def p1_nodes(i):
                if not known(i, 1):
                    pool.wait_ge(c_act, 1)
                if known(i, 1):
                    add_nodes(i - 1)
                node_x1(i)

            def p1_trip(i):
                p1(i)
                p1_nodes(i)
            trips(pool, p1_trip)
            add_nodes(TRIPS - 1)

            pool.wait_ge(p1_done, 1)

            def p2(i):
                for s in range(2):
                    u = 2 * i + s
                    pool.wait_ge(lidx_ok, u + 1)
                    pool.wait_ge(h1e_ok, u + 1)
                    pool.sem_inc(pool_turn)
                    for j in range(TE):
                        pool.indirect_dma_start(
                            out=node_table, out_offset=bass.IndirectOffsetOnAxis(ap=lidx[s][:, j:j + 1], axis=0),
                            in_=h1e[s][:, j, :], in_offset=None,
                            bounds_check=last_node, oob_is_err=False).then_inc(d_sc[s], 16)

            trips(pool, p2)
            for s in range(2):
                pool.wait_ge(d_sc[s], 16 * TE * TRIPS)
            pool.sem_inc(p2_done)

            def gather(v, s):
                pool.wait_ge(sidx_ok, v + 1)
                if known(v, 2):
                    pool.wait_ge(catt_ps, v - 1)
                pool.sem_inc(pool_turn)
                for j in range(TE):
                    pool.indirect_dma_start(
                        out=cat[s][:, j, 0:D], out_offset=None, in_=node_table,
                        in_offset=bass.IndirectOffsetOnAxis(ap=sidx[s][:, j:j + 1], axis=0),
                        bounds_check=last_node, oob_is_err=False).then_inc(d_cat[s], 16)

            def scatter(v, s):
                pool.wait_ge(fidx_ok, v + 1)
                pool.wait_ge(res_ok, v + 1)
                pool.sem_inc(pool_turn)
                for j in range(TE):
                    pool.indirect_dma_start(
                        out=out, out_offset=bass.IndirectOffsetOnAxis(ap=fidx[s][:, j:j + 1], axis=0),
                        in_=res[s][:, j, :], in_offset=None,
                        bounds_check=last_node, oob_is_err=False).then_inc(d_fin[s], 16)

            gather(0, 0)
            gather(1, 1)

            def p3(i):
                for s in range(2):
                    v = 2 * i + s
                    if not (isinstance(i, int) and i == TRIPS - 1):
                        gather(v + 2, s)
                    if known(v, 1):
                        scatter(v - 1, 1 - s)

            p3(0)
            with pool.Fori(1, TRIPS - 1) as i:
                p3(i)
            p3(TRIPS - 1)
            scatter(UNITS - 1, 1)
            for s in range(2):
                pool.wait_ge(d_fin[s], 16 * TE * TRIPS)

        @block.scalar
        def _(act):
            act.wait_ge(d_w, WEIGHT_LOADS)
            act.activation(tanh_b[:, :], tanh_b[:, :], ACT.Tanh).then_inc(c_act, 1)

            def squares_nodes(i, s):
                u = 2 * i + s
                act.wait_ge(ncen_ok, u + 1)
                if known(u, 1):
                    act.wait_ge(nvar_ok, u)
                act.activation(n_sq[:, :, :], h1n[s][:, :, :], ACT.Square, scale=D ** -0.5).then_inc(nsq_ok, 1)

            def squares_edges(i, s):
                u = 2 * i + s
                act.wait_ge(ecen_ok, u + 1)
                if known(u, 1):
                    act.wait_ge(evar_ok, u)
                act.activation(e_sq[:, :, :], e_cen[s][:, :, :], ACT.Square, scale=D ** -0.5).then_inc(esq_ok, 1)
                act.activation(keep[:, ds(u * TE, TE), D:2 * D], xe[s][:, TE:GE, :], ACT.Copy).then_inc(xdst_ok, 1)

            def evacuate(u):
                act.wait_ge(h1t_ps, u + 1)
                if known(u, 1):
                    act.wait_ge(c1_ps, 4 * u)
                act.activation(h1t[:, 0, :], psum[0][:, 0:4 * P], ACT.Copy).then_inc(h1t_ok, 1)
                act.activation(h1t[:, 1, :], psum[1][:, 0:4 * P], ACT.Copy).then_inc(h1t_ok, 1)

            def gelu_hidden(u, quarters):
                for q in quarters:
                    act.wait_ge(c1_ps, 4 * u + q + 1)
                    if q % 2 == 0 and known(u, 1):
                        act.wait_ge(z2_ps, 2 * u - 1 + q // 2)
                    act.activation(c1t[:, q, :], psum[2 + q % 2][0:HC, 0:4 * P], ACT.Gelu,
                                   bias=bc1[:, 0:1]).then_inc(c1_ok, 1)

            def gelu_out(u):
                if known(u, 1):
                    act.wait_ge(g2_ps, u)
                for k in range(2):
                    act.wait_ge(z2_ps, 2 * u + k + 1)
                    act.activation(g2t[:, k, :], psum[4 + k][:, 0:4 * P], ACT.Gelu, bias=bc2[:, 0:1])\
                        .then_inc(g2_ok, 1)

            def p1(i):
                act.wait_ge(nvar_ok, 2 * i + 2)
                act.wait_ge(evar_ok, 2 * i + 2)
                act.activation(std[:, :, :], var[:, :, :], ACT.Sqrt, bias=ln_eps[:, 0:1]).then_inc(std_ok, 1)
                if known(i, 1):
                    gelu_out(2 * i - 1)
                evacuate(2 * i)
                more = not (isinstance(i, int) and i == TRIPS - 1)
                gelu_hidden(2 * i, (0, 1, 2))
                if more:
                    squares_nodes(i + 1, 0)
                gelu_hidden(2 * i, (3,))
                if more:
                    squares_edges(i + 1, 0)
                evacuate(2 * i + 1)
                gelu_out(2 * i)
                if more:
                    squares_nodes(i + 1, 1)
                gelu_hidden(2 * i + 1, (0, 1))
                if more:
                    squares_edges(i + 1, 1)
                gelu_hidden(2 * i + 1, (2, 3))

            for s in range(2):
                squares_nodes(0, s)
                squares_edges(0, s)
            p1(0)
            with act.Fori(1, TRIPS - 1) as i:
                p1(i)
            p1(TRIPS - 1)
            gelu_out(UNITS - 1)

            act.wait_ge(m_step, DIFF_READY)
            act.activation(decay_row[:, :, :], d_row[:, :, :], ACT.Exp).then_inc(m_act, 1)
            act.activation(w_row[:, :, :], z_row[:, :, :], ACT.Exp).then_inc(m_act, 1)

            act.wait_ge(p1_done, 1)

            def p2(i):
                act.wait_ge(att_ok, i + 1)
                if known(i, 1):
                    act.wait_ge(x1_ok, i)
                act.activation(att_th[:, :, :], att_out[:, :, :], ACT.Tanh).then_inc(th_ok, 1)
                act.wait_ge(lcen_ok, i + 1)
                if known(i, 1):
                    act.wait_ge(lvar_ok, i)
                act.activation(l_sq[:, :, :], l_cen[:, :, :], ACT.Square, scale=D ** -0.5).then_inc(lsq_ok, 1)
                act.wait_ge(leps_ok, i + 1)
                if known(i, 1):
                    act.wait_ge(lrstd_ok, i)
                act.activation(keep[:, ds(i * 2 * TE, 2 * TE), D:2 * D], x1_last[:, :, :], ACT.Copy).then_inc(x1k_ok, 1)
                act.activation(l_std[:, :], l_eps[:, :], ACT.Sqrt).then_inc(lstd_ok, 1)
                for s in range(2):
                    u = 2 * i + s
                    act.wait_ge(h1e_ok, u + 1)
                    act.activation(keep[:, ds(u * TE, TE), 0:D], h1e[s][:, :, :], ACT.Copy).then_inc(h1k_ok, 1)

            trips(act, p2)

            def keep_copy(i, s):
                v = 2 * i + s
                if known(v, 2):
                    act.wait_ge(keptt_ps, v - 1)
                act.activation(kept[s][:, :, :], keep[:, ds(mirror(i, s) * TE, TE), :], ACT.Copy).then_inc(kept_ok, 1)

            def gelu_hidden_e(v):
                act.wait_ge(ce_ps, v + 1)
                if known(v, 1):
                    act.wait_ge(ge_ps, v)
                act.activation(c1e[0:HC, :], psum[5][0:HC, 0:UE], ACT.Gelu, bias=bc1[:, 0:1]).then_inc(ce_ok, 1)

            def gelu_out_e(v):
                act.wait_ge(ge_ps, v + 1)
                if known(v, 1):
                    act.wait_ge(res_ok, v)
                act.activation(g3[:, :, :], psum[6][0:P, 0:TE * D].rearrange("p (j d) -> p j d", d=D), ACT.Gelu)\
                    .then_inc(ge_ok, 1)

            act.wait_ge(h1k_ok, UNITS)
            act.wait_ge(x1k_ok, TRIPS)
            keep_copy(0, 0)

            def p3(i):
                for s in range(2):
                    v = 2 * i + s
                    act.wait_ge(catt_ps, v + 1)
                    if known(v, 1):
                        act.wait_ge(m1_ps, v)
                    act.activation(cat_t[:, :], psum[2][0:D + DE, 0:UE], ACT.Copy).then_inc(catt_ok, 1)
                    if known(v, 1):
                        gelu_hidden_e(v - 1)
                    act.wait_ge(m1_ps, v + 1)
                    if known(v, 1):
                        act.wait_ge(m2_ps, v)
                    act.activation(msg_h[:, :], psum[3][0:HM, 0:UE], ACT.Gelu, bias=bm1[:, 0:1]).then_inc(m1_ok, 1)
                    if known(v, 1):
                        gelu_out_e(v - 1)
                    if not (isinstance(i, int) and i == TRIPS - 1 and s == 1):
                        keep_copy(i + s, 1 - s)
                    act.wait_ge(m2_ps, v + 1)
                    if known(v, 1):
                        act.wait_ge(box_ok, v)
                    act.activation(msg[:, :], psum[4][0:D, 0:UE], ACT.Gelu, bias=bm2[:, 0:1]).then_inc(m2_ok, 1)

            p3(0)
            with act.Fori(1, TRIPS - 1) as i:
                p3(i)
            p3(TRIPS - 1)
            gelu_hidden_e(UNITS - 1)
            gelu_out_e(UNITS - 1)

        @block.vector
        def _(dve):
            step = [0]

            def then(ins):
                step[0] += 1
                ins.then_inc(c_step, 1)
                dve.wait_ge(c_step, step[0])

            dve.memset(w0_ext[:, D:D1], 0.0).then_inc(c_step, 1)
            step[0] += 1
            dve.wait_ge(c_step, 1)
            then(dve.memset(w0_ext[D:D1, D:D1], 1.0))
            then(dve.memset(line_m[0:1, 0:1], -BIG))
            then(dve.memset(ln_eps[:, :], LN_EPS))
            dve.wait_ge(d_rows, 16 * (2 + 2 * RB))
            then(dve.tensor_copy(row_dst_f[:, :, :], row_dst[:, :, :]))
            then(dve.tensor_copy(row_src_f[:, :, :], row_src[:, :, :]))
            then(dve.tensor_tensor(same_prev[:, :, :], row_dst_f[:, :, 1:P + 1], row_dst_f[:, :, 0:P], ALU.is_equal))
            then(dve.tensor_tensor(same_next[:, :, :], row_dst_f[:, :, 1:P + 1], row_dst_f[:, :, 2:P + 2], ALU.is_equal))
            assert step[0] == ROWS_READY
            then(dve.tensor_scalar(pen[:, :, :], same_prev[:, :, :], -1.0, BIG, ALU.add, ALU.mult))
            then(dve.tensor_reduce(pen_min[:, :], pen[:, :, :], AX.X, ALU.min))
            dve.wait_ge(c_pe, 1)
            idx_v = gather_idx[:, :, :]
            then(dve.tensor_copy(idx_v[:, :, 0:TE], psum[0][0:P, 0:ET].rearrange("p (u j) -> p u j", j=TE)))
            then(dve.tensor_copy(idx_v[:, :, TE:GE], psum[0][0:P, 256:256 + ET].rearrange("p (u j) -> p u j", j=TE)))

            def stage_idx(u, s):
                dve.tensor_copy(idx_now[s][:, :], gather_idx[:, ds(u, 1), :].rearrange("p a g -> p (a g)"))\
                    .then_inc(idx_ok, 1)

            stage_idx(0, 0)
            stage_idx(1, 1)
            then(dve.tensor_copy(dst_f[:, :], psum[0][0:P, 256:256 + ET]))
            for psum_at, flag, tmp, idx in ((256, last_f, tmp_l, last_idx), (0, first_f, tmp_f, first_idx)):
                then(dve.tensor_scalar(flag[:, :], psum[1][0:P, psum_at:psum_at + ET], -1.0, 1.0, ALU.mult, ALU.add))
                then(dve.tensor_scalar(tmp[:, :], dst_f[:, :], -SKIP, None, ALU.add))
                then(dve.tensor_tensor(tmp[:, :], tmp[:, :], flag[:, :], ALU.mult))
                then(dve.tensor_scalar(idx[:, :], tmp[:, :], SKIP, None, ALU.add))
            dve.wait_ge(ident_ok, 1)
            then(dve.tensor_tensor(stack_id[:, :], ident[:, 0:D], ident[:, D:2 * D], ALU.add))
            dve.wait_ge(c_pe, 2)
            dve.wait_ge(d_w, WEIGHT_LOADS)
            then(dve.tensor_copy(w0_t[:, :], psum[2][0:D, 0:D]))
            then(dve.tensor_copy(att_rep[:, :, :], bcast(att_col[:, :], [D, 2, 128], 2)))
            assert step[0] == ATT_READY
            dve.wait_ge(c_pe, 3)
            for g in range(2):
                then(dve.tensor_copy(att_vec[:, g * TE:(g + 1) * TE, :],
                                     bcast(psum[2][0:P, 64 + g * D:64 + (g + 1) * D], [P, TE, D], 1)))
            dve.wait_ge(c_act, 1)

            def sums(i, s):
                u = 2 * i + s
                dve.wait_ge(d_xe[s], 16 * GE * (i + 1))
                dve.tensor_reduce(e_sum[s][:, :], xe[s][:, :, :], AX.X, ALU.add).then_inc(esum_ok, 1)
                if s == 0:
                    dve.wait_ge(d_xn[s], 32 * (i + 1))
                    if known(i, 1):
                        dve.wait_ge(s1n_ok[s], i)
                    dve.tensor_tensor(x1n[s][:, :, :], xn[s][:, :, :], bcast(tanh_b[:, :], [P, TN, D], 1),
                                      ALU.add).then_inc(nx1_ok[s], 1)
                dve.wait_ge(nx1_ok[s], i + 1)
                dve.tensor_reduce(n_sum[s][:, :], x1n[s][:, :, :], AX.X, ALU.add).then_inc(nsum_ok, 1)

            def centre(i, s):
                u = 2 * i + s
                dve.wait_ge(esum_ok, u + 1)
                dve.scalar_tensor_tensor(out=e_cen[s][:, :, :], in0=bcast(e_sum[s][:, :], [P, GE, D], 2),
                                         scalar=-1.0 / D, in1=xe[s][:, :, :],
                                         op0=ALU.mult, op1=ALU.add).then_inc(ecen_ok, 1)
                if known(u, 2):
                    dve.wait_ge(d_tab[s], 32 * i)
                    dve.wait_ge(h1t_ps, u - 1)
                    dve.wait_ge(s1n_ok[s], i)
                dve.wait_ge(nsum_ok, u + 1)
                dve.scalar_tensor_tensor(out=h1n[s][:, :, :], in0=bcast(n_sum[s][:, :], [P, TN, D], 2),
                                         scalar=-1.0 / D, in1=x1n[s][:, :, :],
                                         op0=ALU.mult, op1=ALU.add).then_inc(ncen_ok, 1)
                if not (isinstance(i, int) and i == TRIPS - 1):
                    stage_idx(u + 2, s)

            def variances(i, s):
                u = 2 * i + s
                dve.wait_ge(nsq_ok, u + 1)
                if s == 0 and known(i, 1):
                    dve.wait_ge(std_ok, i)
                dve.tensor_reduce(var[:, s, 0:TN], n_sq[:, :, :], AX.X, ALU.add).then_inc(nvar_ok, 1)
                dve.wait_ge(esq_ok, u + 1)
                dve.tensor_reduce(var[:, s, TN:], e_sq[:, :, :], AX.X, ALU.add).then_inc(evar_ok, 1)

            def dots(u, s):
                dve.wait_ge(ecen_ok, u + 1)
                if known(u, 1):
                    dve.wait_ge(edot_ok, u)
                dve.scalar_tensor_tensor(out=e_prod[:, :, :], in0=e_cen[s][:, :, :], scalar=0.0,
                                         in1=att_vec[:, :, :], op0=ALU.max, op1=ALU.mult).then_inc(eprod_ok, 1)
                dve.wait_ge(eprod_ok, u + 1)
                dve.tensor_reduce(e_dot[s][:, :], e_prod[:, :, :], AX.X, ALU.add).then_inc(edot_ok, 1)

            def normalise(i, s):
                u = 2 * i + s
                dve.scalar_tensor_tensor(out=h1n[s][:, :, :], in0=h1n[s][:, :, :], scalar=0.0,
                                         in1=bcast(rstd[:, s, 0:TN], [P, TN, D], 2),
                                         op0=ALU.max, op1=ALU.mult).then_inc(h1n_ok, 1)
                dve.wait_ge(edot_ok, u + 1)
                if known(u, 1):
                    dve.wait_ge(logit_ok, u)
                dve.tensor_tensor(e_sc[:, :], e_dot[s][:, :], rstd[:, s, TN:], ALU.mult).then_inc(esc_ok, 1)
                dve.scalar_tensor_tensor(out=keep[:, ds(u * TE, TE), 0:D], in0=e_cen[s][:, 0:TE, :], scalar=0.0,
                                         in1=bcast(rstd[:, s, TN:TN + TE], [P, TE, D], 2),
                                         op0=ALU.max, op1=ALU.mult).then_inc(keeph_ok, 1)
                dve.wait_ge(esc_ok, u + 1)
                dve.tensor_tensor(logit[:, ds(u * TE, TE)], e_sc[:, 0:TE], e_sc[:, TE:GE], ALU.add)\
                    .then_inc(logit_ok, 1)
                if s == 0:
                    dve.wait_ge(h1n_ok, u + 1)
                    dve.tensor_tensor(s1n[s][:, :, :], x1n[s][:, :, :], h1n[s][:, :, :], ALU.add)\
                        .then_inc(s1n_ok[s], 1)

            def p1(i):
                sums(i, 0)
                centre(i, 0)
                sums(i, 1)
                variances(i, 0)
                centre(i, 1)
                dots(2 * i, 0)
                dots(2 * i + 1, 1)
                variances(i, 1)
                if known(i, 1):
                    finish_nodes(i - 1, 0)
                dve.wait_ge(std_ok, i + 1)
                dve.reciprocal(rstd[:, :, :], std[:, :, :]).then_inc(rstd_ok, 1)
                dve.wait_ge(rstd_ok, i + 1)
                if known(i, 1):
                    dve.wait_ge(resn_ok, 2 * i - 1)
                normalise(i, 0)
                normalise(i, 1)
                if known(i, 1):
                    finish_nodes(i - 1, 1)

            def finish_nodes(i, s):
                u = 2 * i + s
                dve.wait_ge(g2_ps, u + 1)
                dve.wait_ge(s1n_ok[s], i + 1)
                if known(i, 1):
                    dve.wait_ge(d_res[s], 32 * i)
                dve.tensor_tensor(resn[s][:, :, :].rearrange("p (b j) d -> p b (j d)", b=2), psum_all[0:P, 6:8, :],
                                  s1n[s][:, :, :].rearrange("p (b j) d -> p b (j d)", b=2), ALU.add)\
                    .then_inc(resn_ok, 1)

            p1(0)
            with dve.Fori(1, TRIPS - 1) as i:
                p1(i)
            p1(TRIPS - 1)
            finish_nodes(TRIPS - 1, 0)
            finish_nodes(TRIPS - 1, 1)

            mark = [0]

            def then_m(ins):
                mark[0] += 1
                ins.then_inc(m_step, 1)
                dve.wait_ge(m_step, mark[0])

            def by_row(bank):
                return psum[bank][0:RR, 0:RB * P].rearrange("r (b p) -> r b p", p=P)

            dve.wait_ge(m_pe, 1)
            then_m(dve.tensor_copy(z_row[:, :, :], by_row(0)))
            then_m(dve.scalar_tensor_tensor(out=e_row[:, :, :], in0=z_row[:, :, :], scalar=SLOPE,
                                            in1=z_row[:, :, :], op0=ALU.mult, op1=ALU.max))
            for b in range(RB):
                then_m(dve.tensor_tensor_scan(m_row[:, b, :], pen[:, b, :], e_row[:, b, :], -BIG, ALU.add, ALU.max))
            assert mark[0] == ROW_MAX_READY
            dve.wait_ge(m_pe, 2)
            then_m(dve.tensor_copy(line[0:1, :], psum[1][0:1, 0:2 * ET]))
            then_m(dve.tensor_tensor_scan(line_m[0:1, 1:ET + 1], line[0:1, ET:2 * ET], line[0:1, 0:ET], -BIG,
                                          ALU.add, ALU.max))
            assert mark[0] == LINE_READY
            dve.wait_ge(m_pe, 3)
            then_m(dve.tensor_copy(m_run[:, :, 0], psum[2][0:RR, 0:RB]))
            for b in range(RB):
                then_m(dve.tensor_tensor_scan(m_run[:, b, 1:P + 1], pen[:, b, :], e_row[:, b, :], m_run[:, b, 0:1],
                                              ALU.add, ALU.max))
            then_m(dve.tensor_tensor(d_row[:, :, :], m_run[:, :, 0:P], m_run[:, :, 1:P + 1], ALU.subtract))
            then_m(dve.tensor_scalar(d_row[:, :, :], d_row[:, :, :], 0.0, None, ALU.min))
            then_m(dve.tensor_tensor(z_row[:, :, :], e_row[:, :, :], m_run[:, :, 1:P + 1], ALU.subtract))
            assert mark[0] == DIFF_READY
            dve.wait_ge(m_act, 1)
            then_m(dve.tensor_tensor(decay_row[:, :, :], decay_row[:, :, :], same_prev[:, :, :], ALU.mult))
            assert mark[0] == DECAY_READY
            dve.wait_ge(m_pe, 4)
            then_m(dve.tensor_copy(weight[:, :], psum[3][0:P, 0:ET]))
            assert mark[0] == SM_DONE

            dve.wait_ge(p1_done, 1)
            dve.memset(acc[1][:, UE - 1:UE], 0.0).then_inc(p2_ready, 1)
            dve.memset(c1e[HC:HC + 1, :], 1.0).then_inc(p2_ready, 1)
            dve.wait_ge(p2_ready, 2)

            def weigh(i):
                if known(i, 1):
                    dve.wait_ge(wht_ps, 2 * i)
                t = ds(i * 2 * TE, 2 * TE)
                dve.tensor_tensor(wh[:, :, 0:D], keep[:, t, 0:D], bcast(weight[:, t], [P, 2 * TE, D], 2),
                                  ALU.mult).then_inc(wh_ok, 1)
                dve.tensor_copy(wh[:, :, D], weight[:, t]).then_inc(whw_ok, 1)

            weigh(0)

            def p2(i):
                t = ds(i * 2 * TE, 2 * TE)
                dve.tensor_tensor(x_last[:, :, :], keep[:, t, D:2 * D], bcast(last_f[:, t], [P, 2 * TE, D], 2),
                                  ALU.mult).then_inc(xlast_ok, 1)
                for s in range(2):
                    u = 2 * i + s
                    dve.wait_ge(wht_ps, u + 1)
                    dve.wait_ge(d_dec[s], 16 * (i + 1))
                    if known(u, 1):
                        dve.wait_ge(acc_ok, u)
                    if known(u, 2):
                        dve.wait_ge(num_ps, u - 1)
                    dve.tensor_tensor_scan(acc[s][:, :], decay[s][:, :], psum[s][0:D1, 0:UE],
                                           acc[1 - s][:, UE - 1:UE], ALU.mult, ALU.add).then_inc(acc_ok, 1)
                dve.wait_ge(num_ps, 2 * i + 2)
                num = psum_all[0:P, 2:4, 0:TE * D1].rearrange("p b (j d) -> p b j d", d=D1)
                dve.tensor_scalar(den_eps[:, :].rearrange("p (b j) -> p b j", b=2), num[:, :, :, D], SM_EPS, None,
                                  ALU.add).then_inc(dene_ok, 1)
                dve.wait_ge(dene_ok, i + 1)
                dve.reciprocal(den_inv[:, :], den_eps[:, :]).then_inc(deni_ok, 1)
                dve.wait_ge(deni_ok, i + 1)
                dve.tensor_tensor(den_last[:, :], den_inv[:, :], last_f[:, t], ALU.mult).then_inc(denl_ok, 1)
                dve.wait_ge(denl_ok, i + 1)
                for s in range(2):
                    ins = dve.tensor_tensor(att_out[:, s * TE:(s + 1) * TE, :], num[:, s, :, 0:D],
                                            bcast(den_last[:, s * TE:(s + 1) * TE], [P, TE, D], 2), ALU.mult)
                ins.then_inc(att_ok, 1)
                if not (isinstance(i, int) and i == TRIPS - 1):
                    weigh(i + 1)
                dve.wait_ge(th_ok, i + 1)
                dve.wait_ge(xlast_ok, i + 1)
                if known(i, 1):
                    dve.wait_ge(x1k_ok, i)
                dve.tensor_tensor(x1_last[:, :, :], x_last[:, :, :], att_th[:, :, :], ALU.add).then_inc(x1_ok, 1)
                dve.wait_ge(x1_ok, i + 1)
                dve.tensor_reduce(l_sum[:, :], x1_last[:, :, :], AX.X, ALU.add).then_inc(lsum_ok, 1)
                dve.wait_ge(lsum_ok, i + 1)
                dve.tensor_scalar(l_mean[:, :], l_sum[:, :], 1.0 / D, None, ALU.mult).then_inc(lmean_ok, 1)
                dve.wait_ge(lmean_ok, i + 1)
                dve.tensor_tensor(l_cen[:, :, :], x1_last[:, :, :], bcast(l_mean[:, :], [P, 2 * TE, D], 2),
                                  ALU.subtract).then_inc(lcen_ok, 1)
                for s in range(2):
                    if known(i, 1):
                        dve.wait_ge(d_sc[s], 16 * TE * i)
                    dve.tensor_copy(lidx[s][:, :], last_idx[:, ds(2 * i * TE + s * TE, TE)]).then_inc(lidx_ok, 1)
                dve.wait_ge(lsq_ok, i + 1)
                dve.tensor_reduce(l_var[:, :], l_sq[:, :, :], AX.X, ALU.add).then_inc(lvar_ok, 1)
                dve.wait_ge(lvar_ok, i + 1)
                dve.tensor_scalar(l_eps[:, :], l_var[:, :], LN_EPS, None, ALU.add).then_inc(leps_ok, 1)
                dve.wait_ge(lstd_ok, i + 1)
                dve.reciprocal(l_rstd[:, :], l_std[:, :]).then_inc(lrstd_ok, 1)
                dve.wait_ge(lrstd_ok, i + 1)
                for s in range(2):
                    if known(i, 1):
                        dve.wait_ge(h1k_ok, 2 * i - 1 + s)
                    dve.scalar_tensor_tensor(out=h1e[s][:, :, :], in0=l_cen[:, s * TE:(s + 1) * TE, :], scalar=0.0,
                                             in1=bcast(l_rstd[:, s * TE:(s + 1) * TE], [P, TE, D], 2),
                                             op0=ALU.max, op1=ALU.mult).then_inc(h1e_ok, 1)

            p2(0)
            with dve.Fori(1, TRIPS - 1) as i:
                p2(i)
            p2(TRIPS - 1)

            def stage_src(i, s):
                v = 2 * i + s
                if known(v, 2):
                    dve.wait_ge(d_cat[s], 16 * TE * i)
                dve.tensor_copy(sidx[s][:, :],
                                gather_idx[:, ds(mirror(i, s), 1), 0:TE].rearrange("p a g -> p (a g)"))\
                    .then_inc(sidx_ok, 1)

            def stage_first(i, s):
                v = 2 * i + s
                if known(v, 2):
                    dve.wait_ge(d_fin[s], 16 * TE * i)
                dve.tensor_copy(fidx[s][:, :], first_idx[:, ds(mirror(i, s) * TE, TE)]).then_inc(fidx_ok, 1)

            def box_sums(v, s):
                dve.wait_ge(m2_ok, v + 1)
                if known(v, 1):
                    dve.wait_ge(box_ok, v)
                if known(v, 2):
                    dve.wait_ge(ce_ps, v - 1)
                dve.tensor_tensor_scan(box[s][:, ::-1], same[s][0:D, ::-1], msg[:, ::-1],
                                       box[1 - s][:, 0:1], ALU.mult, ALU.add).then_inc(box_ok, 1)

            def finish_edges(i, s):
                v = 2 * i + s
                dve.wait_ge(ge_ok, v + 1)
                stage_first(i, s)
                dve.tensor_tensor(res[s][:, :, :], g3[:, :, :],
                                  psum[6][0:P, 256:512].rearrange("p (j d) -> p j d", d=D), ALU.add)\
                    .then_inc(res_ok, 1)

            dve.memset(fill[1][:, 0:1], 0.0).then_inc(p2_ready, 1)
            dve.memset(box[1][:, 0:1], 0.0).then_inc(p2_ready, 1)
            dve.wait_ge(p2_ready, 4)
            stage_src(0, 0)
            stage_src(0, 1)

            def p3(i):
                for s in range(2):
                    v = 2 * i + s
                    if known(v, 1):
                        box_sums(v - 1, 1 - s)
                    dve.wait_ge(keptt_ps, v + 1)
                    dve.wait_ge(d_same[s], 16 * (i + 1))
                    if known(v, 1):
                        dve.wait_ge(fill_ok, v)
                    if known(v, 2):
                        dve.wait_ge(ge_ps, v - 1)
                    dve.tensor_tensor_scan(fill[s][:, ::-1], same[s][:, ::-1], psum[s][:, UE - 1::-1],
                                           fill[1 - s][:, 0:1], ALU.mult, ALU.add).then_inc(fill_ok, 1)
                    if not (isinstance(i, int) and i == TRIPS - 1):
                        stage_src(i + 1, s)
                    if known(v, 1):
                        finish_edges(i - 1 + s, 1 - s)

            p3(0)
            with dve.Fori(1, TRIPS - 1) as i:
                p3(i)
            p3(TRIPS - 1)
            box_sums(UNITS - 1, 1)
            finish_edges(TRIPS - 1, 1)

        @block.tensor
        def _(pe):
            pe.wait_ge(ident_ok, 1)
            pe.wait_ge(c_step, ROWS_READY)
            for b in range(RB):
                pe.transpose(psum[0][0:P, b * RR:(b + 1) * RR], row_src_f[:, b, :], ident[0:RR, 0:RR])
                pe.transpose(psum[0][0:P, 256 + b * RR:256 + (b + 1) * RR], row_dst_f[:, b, 1:P + 1], ident[0:RR, 0:RR])
                pe.transpose(psum[1][0:P, b * RR:(b + 1) * RR], same_prev[:, b, :], ident[0:RR, 0:RR])
                last = pe.transpose(psum[1][0:P, 256 + b * RR:256 + (b + 1) * RR], same_next[:, b, :], ident[0:RR, 0:RR])
            last.then_inc(c_pe, 1)
            pe.wait_ge(d_w, WEIGHT_LOADS)
            pe.transpose(psum[2][0:D, 0:D], w0_ext[0:D, 0:D], ident[0:D, 0:D]).then_inc(c_pe, 1)
            pe.wait_ge(c_step, ATT_READY)
            for g in range(2):
                last = pe.matmul(psum[2][:, 64 + g * D:64 + (g + 1) * D], att_rep[:, g, :], w0_t[:, :],
                                 start=True, stop=True)
            last.then_inc(c_pe, 1)

            def out_layer(u):
                for k in range(2):
                    if known(u, 1):
                        pe.wait_ge(g2_ok, 2 * u - 1 + k)
                    for q in range(2):
                        pe.wait_ge(c1_ok, 4 * u + 2 * k + q + 1)
                        last = pe.matmul(psum[4 + k][q * D:(q + 1) * D, 0:4 * P], wc2_ext[0:HC, :],
                                         c1t[:, 2 * k + q, :], start=True, stop=True)
                    last.then_inc(z2_ps, 1)

            def turn_back(u):
                if known(u, 1):
                    pe.wait_ge(resn_ok, u)
                for c in range(TN // 2):
                    if c % 4 == 0:
                        pe.wait_ge(g2_ok, 2 * u + c // 4 + 1)
                    last = pe.transpose(psum[6 + c // 4][0:P, (c % 4) * 2 * D:(c % 4 + 1) * 2 * D],
                                        g2t[:, c // 4, (c % 4) * P:(c % 4 + 1) * P], ident[:, :])
                last.then_inc(g2_ps, 1)

            def turn(u, s):
                pe.wait_ge(h1n_ok, u + 1)
                if known(u, 1):
                    pe.wait_ge(h1t_ok, 2 * u)
                for c in range(TN // 2):
                    last = pe.transpose(psum[c // 4][:, (c % 4) * P:(c % 4 + 1) * P],
                                        h1n[s][:, 2 * c:2 * c + 2, :].rearrange("p j d -> p (j d)"),
                                        ident[0:P, 0:P])
                last.then_inc(h1t_ps, 1)

            def hidden_layer(u, halves=(0, 1)):
                for k in halves:
                    pe.wait_ge(h1t_ok, 2 * u + k + 1)
                    for q in range(2):
                        if known(4 * u + 2 * k + q, 2):
                            pe.wait_ge(c1_ok, 4 * u + 2 * k + q - 1)
                        pe.matmul(psum[2 + q][0:HC, 0:4 * P], wc1_top[q * D:(q + 1) * D, :],
                                  h1t[q * D:(q + 1) * D, k, :], start=True, stop=True).then_inc(c1_ps, 1)

            def p1(i):
                if known(i, 1):
                    turn_back(2 * i - 1)
                turn(2 * i, 0)
                hidden_layer(2 * i)
                turn(2 * i + 1, 1)
                out_layer(2 * i)
                hidden_layer(2 * i + 1, (0,))
                turn_back(2 * i)
                hidden_layer(2 * i + 1, (1,))
                out_layer(2 * i + 1)

            pe.wait_ge(c_step, CONST_READY)
            trips(pe, p1)
            turn_back(UNITS - 1)

            pe.wait_ge(logit_ok, UNITS)
            pe.wait_ge(h1t_ok, 2 * UNITS)
            pe.wait_ge(c1_ok, 4 * UNITS)
            for b in range(RB):
                last = pe.transpose(psum[0][0:RR, b * P:(b + 1) * P], logit[:, b * RR:(b + 1) * RR], ident[0:P, 0:P])
            last.then_inc(m_pe, 1)
            pe.wait_ge(m_step, ROW_MAX_READY)
            for b in range(RB):
                pe.transpose(psum[1][0:1, b * RR:(b + 1) * RR], m_row[:, b, P - 1:P], ident[0:RR, 0:RR])
                last = pe.transpose(psum[1][0:1, ET + b * RR:ET + (b + 1) * RR], pen_min[:, b:b + 1],
                                    ident[0:RR, 0:RR])
            last.then_inc(m_pe, 1)
            pe.wait_ge(m_step, LINE_READY)
            for b in range(RB):
                last = pe.transpose(psum[2][0:RR, b:b + 1], line_m[0:1, b * RR:(b + 1) * RR], ident[0:1, 0:1])
            last.then_inc(m_pe, 1)
            pe.wait_ge(m_act, 2)
            for b in range(RB):
                last = pe.transpose(psum[3][0:P, b * RR:(b + 1) * RR], w_row[:, b, :], ident[0:RR, 0:RR])
            last.then_inc(m_pe, 1)

            pe.wait_ge(p1_done, 1)

            def p2(i):
                for s in range(2):
                    u = 2 * i + s
                    if s == 0:
                        pe.wait_ge(wh_ok, i + 1)
                        pe.wait_ge(whw_ok, i + 1)
                    if known(u, 2):
                        pe.wait_ge(acc_ok, u - 1)
                    for j in range(TE):
                        last = pe.transpose(psum[s][0:D1, j * P:(j + 1) * P], wh[:, s * TE + j, :], ident[0:P, 0:P])
                    last.then_inc(wht_ps, 1)
                for s in range(2):
                    u = 2 * i + s
                    pe.wait_ge(acc_ok, u + 1)
                    if s == 0 and known(i, 1):
                        pe.wait_ge(att_ok, i)
                    for j in range(TE):
                        last = pe.matmul(psum[2 + s][0:P, j * D1:(j + 1) * D1], acc[s][:, j * P:(j + 1) * P],
                                         w0_ext[:, :], start=True, stop=True)
                    last.then_inc(num_ps, 1)

            trips(pe, p2)

            def turn_edges(v, s, i):
                pe.wait_ge(kept_ok, v + 1)
                if known(v, 2):
                    pe.wait_ge(fill_ok, v - 1)
                for j in range(TE):
                    last = pe.transpose(psum[s][:, j * P:(j + 1) * P], kept[s][:, j, :], ident[0:P, 0:P])
                last.then_inc(keptt_ps, 1)
                pe.wait_ge(d_cat[s], 16 * TE * (i + 1))
                pe.wait_ge(d_ea[s], 16 * (i + 1))
                if known(v, 1):
                    pe.wait_ge(catt_ok, v)
                for j in range(TE):
                    last = pe.transpose(psum[2][0:D + DE, j * P:(j + 1) * P], cat[s][:, j, :], ident[0:P, 0:P])
                last.then_inc(catt_ps, 1)

            def node_hidden(v, s):
                pe.wait_ge(box_ok, v + 1)
                if known(v, 1):
                    pe.wait_ge(ce_ok, v)
                pe.matmul(psum[5][0:HC, 0:UE], wc1_top[0:D, :], fill[s][0:D, :], start=True, stop=False)
                pe.matmul(psum[5][0:HC, 0:UE], wc1_box[:, :], box[s][:, :], start=False, stop=True).then_inc(ce_ps, 1)

            def node_out(v, s):
                pe.wait_ge(ce_ok, v + 1)
                if known(v, 1):
                    pe.wait_ge(res_ok, v)
                for j in range(TE):
                    pe.matmul(psum[6][0:P, j * D:(j + 1) * D], c1e[:, j * P:(j + 1) * P], wc2_ext[:, :],
                              start=True, stop=True)
                for j in range(TE):
                    last = pe.matmul(psum[6][0:P, 256 + j * D:256 + (j + 1) * D], fill[s][:, j * P:(j + 1) * P],
                                     stack_id[:, :], start=True, stop=True)
                last.then_inc(ge_ps, 1)

            def p3(i):
                for s in range(2):
                    v = 2 * i + s
                    turn_edges(v, s, i)
                    if known(v, 1):
                        node_hidden(v - 1, 1 - s)
                    pe.wait_ge(catt_ok, v + 1)
                    pe.wait_ge(fill_ok, v + 1)
                    if known(v, 1):
                        pe.wait_ge(m1_ok, v)
                    pe.matmul(psum[3][0:HM, 0:UE], wm1_src[:, :], cat_t[:, :], start=True, stop=False)
                    pe.matmul(psum[3][0:HM, 0:UE], wm1_dst[:, :], fill[s][0:D, :], start=False, stop=True)\
                        .then_inc(m1_ps, 1)
                    if known(v, 1):
                        node_out(v - 1, 1 - s)
                    pe.wait_ge(m1_ok, v + 1)
                    if known(v, 1):
                        pe.wait_ge(m2_ok, v)
                    pe.matmul(psum[4][0:D, 0:UE], wm2[:, :], msg_h[:, :], start=True, stop=True).then_inc(m2_ps, 1)

            trips(pe, p3)
            node_hidden(UNITS - 1, 1)
            node_out(UNITS - 1, 1)


WEIGHT_LOADS = 16 * 19
ROWS_READY = 8
ATT_READY = 24
CONST_READY = 26
ROW_MAX_READY = 4
LINE_READY = 6
DIFF_READY = 12
DECAY_READY = 13
SM_DONE = 14

_INS = ['x', 'src', 'dst', 'edge_attr_32', 'L0_gnn_W', 'L0_gnn_att_src', 'L0_gnn_att_dst', 'L0_gnn_bias',
        'L1_gnn_W_m1', 'L1_gnn_b_m1', 'L1_gnn_W_m2', 'L1_gnn_b_m2', 'L1_gnn_W_c1', 'L1_gnn_b_c1', 'L1_gnn_W_c2',
        'L1_gnn_b_c2']
_OUTS = [((100000, 64), 'float32')]


def kernel(**inputs):
    import numpy as _np
    import concourse.bacc as _bacc
    from concourse import mybir as _mybir
    from concourse.bass_utils import run_bass_kernel_spmd as _run

    nc = _bacc.Bacc("TRN2", target_bir_lowering=False, num_devices=1)
    arrays, args = {}, []
    for name in _INS:
        a = _np.ascontiguousarray(inputs[name])
        arrays[f"in_{name}_dram"] = a
        args.append(nc.dram_tensor(f"in_{name}_dram", a.shape, _mybir.dt.from_np(a.dtype), kind="ExternalInput").ap())
    for i, (shape, dtype) in enumerate(_OUTS):
        dt = _mybir.dt.from_np(_np.dtype(dtype))
        args.append(nc.dram_tensor(f"out_{i}_dram", shape, dt, kind="ExternalOutput").ap())
    gnn_two_layer_kernel(nc, *args)
    r = _run(nc, [arrays], core_ids=[0])
    return r.results[0]["out_0_dram"]
```

```python
import concourse.bass as bass
from concourse import mybir
from contextlib import ExitStack


def gnn_two_layer_kernel(
    nc: bass.Bass,
    x: bass.AP,
    src: bass.AP,
    dst: bass.AP,
    edge_attr: bass.AP,
    W0: bass.AP,
    att_src: bass.AP,
    att_dst: bass.AP,
    bias0: bass.AP,
    W_m1: bass.AP,
    b_m1: bass.AP,
    W_m2: bass.AP,
    b_m2: bass.AP,
    W_c1: bass.AP,
    b_c1: bass.AP,
    W_c2: bass.AP,
    b_c2: bass.AP,
    out: bass.AP,
):
    fp32 = mybir.dt.float32
    i32 = mybir.dt.int32
    ALU = mybir.AluOpType
    ACT = mybir.ActivationFunctionType
    AX = mybir.AxisListType
    ds = bass.ds

    N, D = x.shape
    E = src.shape[0]
    DE = edge_attr.shape[1]
    HM = W_m1.shape[1]
    HC = W_c1.shape[1]
    P = 125
    ET = E // P
    TE = 4
    UNITS = ET // TE
    UE = TE * P
    TN = N // UNITS // P
    UN = TN * P
    GE = 2 * TE
    RB = 2
    RR = ET // RB
    PM = 120
    LN_EPS = 1e-5
    SM_EPS = 1e-16
    SLOPE = 0.2
    BIG = 1.0e30
    SKIP = float(1 << 20)
    D1 = D + 1
    TRIPS = UNITS // 2
    assert E == ET * P and ET == UNITS * TE and N == UNITS * UN and UNITS % 2 == 0

    node_table = nc.dram_tensor("node_table", [N, D], fp32).ap()
    decay_dram = nc.dram_tensor("decay_dram", [E], fp32).ap()
    same_dram = nc.dram_tensor("same_dram", [E], fp32).ap()

    def known(u, least):
        return not isinstance(u, int) or u >= least

    def mirror(i, s):
        return i * -2 + (UNITS - 1 - s)

    def bcast(ap, shape, axis):
        return ap.unsqueeze(axis).broadcast_to(shape)

    def rows_of(dram):
        return dram.rearrange("(b r p) -> r b p", b=RB, p=P)

    ctx = ExitStack()
    first_phase = ExitStack()
    with ctx:
        scope = [ctx]

        def sb(name, shape, dt=fp32):
            return scope[0].enter_context(nc.sbuf_tensor(name, shape, dt))

        def sem(name):
            return ctx.enter_context(nc.semaphore(name))

        def two(name, shape, dt=fp32):
            return [sb(f"{name}{s}", shape, dt) for s in range(2)]

        def four(name, shape, dt=fp32):
            return [sb(f"{name}{s}", shape, dt) for s in range(4)]

        ident = sb("ident", [128, 128])
        w0_ext = sb("w0_ext", [D1, D1])
        w0_t = sb("w0_t", [D, D])
        att_col = sb("att_col", [D, 2])
        att_rep = sb("att_rep", [D, 2, 128])
        att_vec = sb("att_vec", [P, GE, D])
        tanh_b = sb("tanh_b", [P, D])
        wc1_h = sb("wc1_h", [D, HC])
        wc1_bh = sb("wc1_bh", [2 * D, HC])
        wc2 = sb("wc2", [HC, D])
        wm1_dst = sb("wm1_dst", [2 * D, HM])
        wm1_src = sb("wm1_src", [D + DE, HM])
        wm2 = sb("wm2", [HM, D])
        ln_eps = sb("ln_eps", [P, 1])
        bc1 = sb("bc1", [HC, 1])
        bc2 = sb("bc2", [2 * D, 1])
        bm1 = sb("bm1", [HM, 1])
        bm2 = sb("bm2", [D, 1])
        row_dst = sb("row_dst", [RR, RB, P + 2], i32)
        row_src = sb("row_src", [RR, RB, P], i32)
        row_dst_f = sb("row_dst_f", [RR, RB, P + 2])
        row_src_f = sb("row_src_f", [RR, RB, P])
        same_prev = sb("same_prev", [RR, RB, P])
        same_next = sb("same_next", [RR, RB, P])
        gather_idx = sb("gather_idx", [P, UNITS, GE], i32)
        dst_f = sb("dst_f", [P, ET])
        last_f = sb("last_f", [P, ET])
        first_f = sb("first_f", [P, ET])
        tmp_l = sb("tmp_l", [P, ET])
        tmp_f = sb("tmp_f", [P, ET])
        last_idx = sb("last_idx", [P, ET], i32)
        first_idx = sb("first_idx", [P, ET], i32)
        keep = sb("keep", [P, ET, 2 * D])
        logit = sb("logit", [P, ET])
        weight = sb("weight", [P, ET])
        scope[0] = first_phase
        idx_now = two("idx_now", [P, GE], i32)
        xe = two("xe", [P, GE, D])
        e_sum = two("e_sum", [P, GE])
        e_cen = two("e_cen", [P, GE, D])
        e_sq = sb("e_sq", [P, GE, D])
        e_prod = sb("e_prod", [P, GE, D])
        e_sc = sb("e_sc", [P, GE])
        e_dot = two("e_dot", [P, GE])
        xn = two("xn", [P, TN, D])
        x1n = two("x1n", [P, TN, D])
        n_sum = two("n_sum", [P, TN])
        n_sq = sb("n_sq", [P, TN, D])
        h1n = two("h1n", [P, TN, D])
        s1n = two("s1n", [P, TN, D])
        h1t = sb("h1t", [128, 2, 4 * P])
        c1t = sb("c1t", [HC, 4, 4 * P])
        g2t = sb("g2t", [2 * D, 2, 4 * P])
        resn = two("resn", [P, TN, D])
        var = sb("var", [P, 2, TN + GE])
        std = sb("std", [P, 2, TN + GE])
        rstd = sb("rstd", [P, 2, TN + GE])
        pen = sb("pen", [RR, RB, P])
        pen_min = sb("pen_min", [RR, RB])
        z_row = sb("z_row", [RR, RB, P])
        e_row = sb("e_row", [RR, RB, P])
        m_row = sb("m_row", [RR, RB, P])
        m_run = sb("m_run", [RR, RB, P + 1])
        line = sb("line", [1, 2 * ET])
        line_m = sb("line_m", [1, ET + 1])
        d_row = sb("d_row", [RR, RB, P])
        decay_row = sb("decay_row", [RR, RB, P])
        w_row = sb("w_row", [RR, RB, P])
        first_phase.close()
        scope[0] = ctx
        wh = sb("wh", [P, 2 * TE, D1])
        decay = two("decay", [D1, UE])
        acc = two("acc", [D1, UE])
        lidx = four("lidx", [P, TE], i32)
        x_last = sb("x_last", [P, 2 * TE, D])
        den_eps = sb("den_eps", [P, 2 * TE])
        den_inv = sb("den_inv", [P, 2 * TE])
        den_last = sb("den_last", [P, 2 * TE])
        att_out = sb("att_out", [P, 2 * TE, D])
        x1_last = sb("x1_last", [P, 2 * TE, D])
        att_th = sb("att_th", [P, 2 * TE, D])
        l_sum = sb("l_sum", [P, 2 * TE])
        l_cen = sb("l_cen", [P, 2 * TE, D])
        l_sq = sb("l_sq", [P, 2 * TE, D])
        l_var = sb("l_var", [P, 2 * TE])
        l_std = sb("l_std", [P, 2 * TE])
        l_rstd = sb("l_rstd", [P, 2 * TE])
        h1e = four("h1e", [P, TE, D])
        sidx = two("sidx", [P, TE], i32)
        fidx = two("fidx", [P, TE], i32)
        cat = two("cat", [P, TE, D + DE])
        kept = two("kept", [P, TE, 2 * D])
        cat_t = sb("cat_t", [D + DE, UE])
        same = two("same", [2 * D, UE])
        fill = two("fill", [2 * D, UE])
        pair = two("pair", [2 * D, UE])
        msg_h = sb("msg_h", [HM, UE])
        msg = sb("msg", [D, UE])
        c1e = sb("c1e", [HC, UE])
        g3t = sb("g3t", [D, UE])
        h1_row = sb("h1_row", [P, TE, D])
        res = two("res", [P, TE, D])

        psum_all = ctx.enter_context(nc.psum_tensor("psum_all", [128, 8, 512], fp32))
        psum = [psum_all[:, i, :] for i in range(8)]

        d_pad = sem("d_pad")
        sp_turn = sem("sp_turn")
        pool_turn = sem("pool_turn")
        d_rows = sem("d_rows")
        d_w = sem("d_w")
        ident_z = sem("ident_z")
        ident_ok = sem("ident_ok")
        c_step = sem("c_step")
        c_pe = sem("c_pe")
        c_act = sem("c_act")
        tables = sem("tables")
        idx_ok = sem("idx_ok")
        d_xe = [sem(f"d_xe{s}") for s in range(2)]
        esum_ok = sem("esum_ok")
        ecen_ok = sem("ecen_ok")
        esq_ok = sem("esq_ok")
        evar_ok = sem("evar_ok")
        std_ok = sem("std_ok")
        rstd_ok = sem("rstd_ok")
        eprod_ok = sem("eprod_ok")
        edot_ok = sem("edot_ok")
        esc_ok = sem("esc_ok")
        keeph_ok = sem("keeph_ok")
        logit_ok = sem("logit_ok")
        xdst_ok = sem("xdst_ok")
        d_xn = [sem(f"d_xn{s}") for s in range(2)]
        nx1_ok = [sem(f"nx1_ok{s}") for s in range(2)]
        nsum_ok = sem("nsum_ok")
        ncen_ok = sem("ncen_ok")
        nsq_ok = sem("nsq_ok")
        nvar_ok = sem("nvar_ok")
        h1n_ok = sem("h1n_ok")
        s1n_ok = [sem(f"s1n_ok{s}") for s in range(2)]
        h1t_ps = sem("h1t_ps")
        h1t_ok = sem("h1t_ok")
        c1_ps = sem("c1_ps")
        c1_ok = sem("c1_ok")
        z2_ps = sem("z2_ps")
        g2_ok = sem("g2_ok")
        g2_ps = sem("g2_ps")
        resn_ok = sem("resn_ok")
        d_tab = [sem(f"d_tab{s}") for s in range(2)]
        d_res = [sem(f"d_res{s}") for s in range(2)]
        m_step = sem("m_step")
        m_pe = sem("m_pe")
        m_act = sem("m_act")
        d_flow = sem("d_flow")

        p1_done = sem("p1_done")
        p2_ready = sem("p2_ready")
        wh_ok = sem("wh_ok")
        whw_ok = sem("whw_ok")
        wht_ps = sem("wht_ps")
        d_dec = [sem(f"d_dec{s}") for s in range(2)]
        acc_ok = sem("acc_ok")
        num_ps = sem("num_ps")
        xlast_ok = sem("xlast_ok")
        dene_ok = sem("dene_ok")
        deni_ok = sem("deni_ok")
        denl_ok = sem("denl_ok")
        att_ok = sem("att_ok")
        th_ok = sem("th_ok")
        x1_ok = sem("x1_ok")
        x1k_ok = sem("x1k_ok")
        lsum_ok = sem("lsum_ok")
        lcen_ok = sem("lcen_ok")
        lsq_ok = sem("lsq_ok")
        lvar_ok = sem("lvar_ok")
        lstd_ok = sem("lstd_ok")
        lrstd_ok = sem("lrstd_ok")
        h1e_ok = sem("h1e_ok")
        h1k_ok = sem("h1k_ok")
        lidx_ok = sem("lidx_ok")
        d_sc = [sem(f"d_sc{s}") for s in range(4)]
        p2_done = sem("p2_done")
        sidx_ok = sem("sidx_ok")
        fidx_ok = sem("fidx_ok")
        d_cat = [sem(f"d_cat{s}") for s in range(2)]
        d_ea = [sem(f"d_ea{s}") for s in range(2)]
        d_same = [sem(f"d_same{s}") for s in range(2)]
        kept_ok = sem("kept_ok")
        catt_ps = sem("catt_ps")
        catt_ok = sem("catt_ok")
        keptt_ps = sem("keptt_ps")
        fill_ok = sem("fill_ok")
        pairh_ok = sem("pairh_ok")
        m1_ps = sem("m1_ps")
        m1_ok = sem("m1_ok")
        m2_ps = sem("m2_ps")
        m2_ok = sem("m2_ok")
        box_ok = sem("box_ok")
        ce_ps = sem("ce_ps")
        ce_ok = sem("ce_ok")
        ge_ps = sem("ge_ps")
        ge_ok = sem("ge_ok")
        sum_ok = sem("sum_ok")
        fin_ps = sem("fin_ps")
        h1row_ok = sem("h1row_ok")
        res_ok = sem("res_ok")
        d_fin = [sem(f"d_fin{s}") for s in range(2)]

        block = ctx.enter_context(nc.Block())

        def paired_trips(eng, trip):
            for i in range(3):
                trip(i, i % 2, i // 2)
            with eng.Fori(1, (TRIPS - 3) // 2) as j:
                trip(j * 2 + 1, 1, j)
                trip(j * 2 + 2, 0, j + 1)
            for i in (TRIPS - 2, TRIPS - 1):
                trip(i, i % 2, i // 2)

        assert TRIPS % 2 == 1

        def last_trip(i):
            return isinstance(i, int) and i == TRIPS - 1

        def trips(eng, trip):
            trip(0)
            with eng.Fori(1, TRIPS) as i:
                trip(i)

        @block.sync
        def _(sp):
            with nc.allow_non_contiguous_dma(reason="one neighbour per row of 125 destinations"):
                sp.wait_ge(d_pad, 1)
                sp.dma_start(row_dst[:, :, 1:P + 1], rows_of(dst)).then_inc(d_rows, 16)
                sp.dma_start(row_src[:, :, :], rows_of(src)).then_inc(d_rows, 16)
                before = dst[P - 1:E].rearrange("(t o) -> t o", o=1)
                after = dst[P:E].rearrange("(t o) -> t o", o=1)
                for b in range(RB):
                    lo = 1 if b == 0 else 0
                    hi = RR if b < RB - 1 else RR - 1
                    t0 = b * RR + lo - 1
                    sp.dma_start(row_dst[lo:RR, b, 0:1],
                                 before[P * t0:P * (t0 + RR - lo - 1) + 1:P, :]).then_inc(d_rows, 16)
                    sp.dma_start(row_dst[0:hi, b, P + 1:P + 2],
                                 after[P * b * RR:P * (b * RR + hi - 1) + 1:P, :]).then_inc(d_rows, 16)
            for to, frm in (
                (w0_ext[0:D, 0:D], W0), (w0_ext[D:D1, 0:D], bias0.unsqueeze(0)),
                (att_col[:, 0:1], att_src.unsqueeze(1)), (att_col[:, 1:2], att_dst.unsqueeze(1)),
                (tanh_b[:, :], bias0.partition_broadcast(P)),
                (wc1_h[:, :], W_c1[0:D, :]), (wc1_bh[D:2 * D, :], W_c1[0:D, :]),
                (wc1_bh[0:D, :], W_c1[D:2 * D, :]), (wc2[:, :], W_c2),
                (wm1_src[0:D, :], W_m1[0:D, :]), (wm1_dst[D:2 * D, :], W_m1[D:2 * D, :]),
                (wm1_src[D:D + DE, :], W_m1[2 * D:2 * D + DE, :]), (wm2[:, :], W_m2),
                (bc1[:, :], b_c1.unsqueeze(1)), (bm1[:, :], b_m1.unsqueeze(1)),
                (bc2[0:D, :], b_c2.unsqueeze(1)), (bc2[D:2 * D, :], b_c2.unsqueeze(1)), (bm2[:, :], b_m2.unsqueeze(1)),
            ):
                sp.dma_start(to, frm).then_inc(d_w, 16)

            def nodes(dram, u):
                return dram[ds(u * UN, UN), :].rearrange("(p j) d -> p j d", j=TN)

            def load(u, s):
                for a, b in ((0, PM), (PM, P)):
                    sp.dma_start(xn[s][a:b, :, :], nodes(x, u)[a:b]).then_inc(d_xn[s], 16)

            load(0, 0)
            load(1, 1)

            def store_table(u, s):
                sp.wait_ge(h1n_ok, u + 1)
                for a, b in ((0, PM), (PM, P)):
                    sp.dma_start(nodes(node_table, u)[a:b], h1n[s][a:b, :, :]).then_inc(d_tab[s], 16)

            def store_result(u, s):
                sp.wait_ge(resn_ok, u + 1)
                for a, b in ((0, PM), (PM, P)):
                    sp.dma_start(nodes(out, u)[a:b], resn[s][a:b, :, :]).then_inc(d_res[s], 16)

            def p1(i):
                for s in range(2):
                    if not (isinstance(i, int) and i == TRIPS - 1):
                        sp.wait_ge(nx1_ok[s], i + 1)
                        load(2 * i + s + 2, s)
                if known(i, 1):
                    store_result(2 * i - 2, 0)
                for s in range(2):
                    store_table(2 * i + s, s)
                if known(i, 1):
                    store_result(2 * i - 1, 1)

            p1(0)
            with sp.Fori(1, TRIPS - 1) as i:
                p1(i)
            p1(TRIPS - 1)
            for s in range(2):
                store_result(UNITS - 2 + s, s)

            sp.dma_start(rows_of(same_dram), same_next[:, :, :]).then_inc(d_flow, 16)
            sp.wait_ge(m_step, DECAY_READY)
            sp.dma_start(rows_of(decay_dram), decay_row[:, :, :]).then_inc(d_flow, 16)
            sp.wait_ge(d_flow, 32)
            for s in range(2):
                sp.wait_ge(d_tab[s], 32 * TRIPS)
                sp.wait_ge(d_res[s], 32 * TRIPS)
            sp.wait_ge(m_step, SM_DONE)
            sp.sem_inc(p1_done)

            def load_decay(u, s):
                sp.dma_start(decay[s][:, :], decay_dram[ds(u * UE, UE)].partition_broadcast(D1)).then_inc(d_dec[s], 16)

            def p2(i):
                for s in range(2):
                    u = 2 * i + s
                    if known(u, 2):
                        sp.wait_ge(acc_ok, u - 1)
                        sp.sem_inc(sp_turn)
                    load_decay(u, s)

            trips(sp, p2)

            def load_edges(i, s):
                e0 = mirror(i, s) * UE
                sp.dma_start(same[s][:, :], same_dram[ds(e0, UE)].partition_broadcast(128)).then_inc(d_same[s], 16)
                sp.dma_start(cat[s][:, :, D:D + DE], edge_attr[ds(e0, UE), :].rearrange("(j p) d -> p j d", p=P))\
                    .then_inc(d_ea[s], 16)

            def p3(i):
                for s in range(2):
                    v = 2 * i + s
                    if known(v, 2):
                        sp.wait_ge(box_ok, v - 1)
                        sp.wait_ge(catt_ps, v - 1)
                        sp.sem_inc(sp_turn)
                    load_edges(i, s)

            trips(sp, p3)

        @block.gpsimd
        def _(pool):
            pool.memset(row_dst[:, :, :], -1).then_inc(d_pad, 1)
            pool.memset(ident[:, :], 0.0).then_inc(ident_z, 1)
            pool.wait_ge(ident_z, 1)
            pool.affine_select(out=ident[:, :], in_=ident[:, :], compare_op=ALU.not_equal, fill=1.0,
                               base=0, pattern=[[-1, 128]], channel_multiplier=1).then_inc(ident_ok, 1)

            last_node = pool.to_reg(N - 1)

            def p1(i):
                for s in range(2):
                    u = 2 * i + s
                    pool.wait_ge(idx_ok, u + 1)
                    if known(u, 2):
                        pool.wait_ge(ecen_ok, u - 1)
                        pool.wait_ge(xdst_ok, u - 1)
                    pool.sem_inc(pool_turn)
                    for g in range(GE):
                        pool.indirect_dma_start(
                            out=xe[s][:, g, :], out_offset=None, in_=x,
                            in_offset=bass.IndirectOffsetOnAxis(ap=idx_now[s][:, g:g + 1], axis=0),
                            bounds_check=last_node, oob_is_err=False).then_inc(d_xe[s], 16)


            def node_x1(i):
                pool.wait_ge(d_xn[1], 32 * (i + 1))
                if known(i, 1):
                    pool.wait_ge(s1n_ok[1], i)
                pool.tensor_tensor(x1n[1][:, :, :], xn[1][:, :, :], bcast(tanh_b[:, :], [P, TN, D], 1), ALU.add)\
                    .then_inc(nx1_ok[1], 1)

            def add_nodes(i):
                pool.wait_ge(h1n_ok, 2 * i + 2)
                if known(i, 1):
                    pool.wait_ge(resn_ok, 2 * i)
                pool.tensor_tensor(s1n[1][:, :, :], x1n[1][:, :, :], h1n[1][:, :, :], ALU.add).then_inc(s1n_ok[1], 1)

            def p1_nodes(i):
                if not known(i, 1):
                    pool.wait_ge(c_act, 1)
                if known(i, 1):
                    add_nodes(i - 1)
                node_x1(i)

            def p1_trip(i):
                p1(i)
                p1_nodes(i)
            trips(pool, p1_trip)
            add_nodes(TRIPS - 1)

            pool.wait_ge(p1_done, 1)

            def p2(i, parity, n):
                for s in range(2):
                    u, slot = 2 * i + s, 2 * parity + s
                    pool.wait_ge(lidx_ok, u + 1)
                    pool.wait_ge(h1e_ok, u + 1)
                    pool.sem_inc(pool_turn)
                    for j in range(TE):
                        pool.indirect_dma_start(
                            out=node_table, out_offset=bass.IndirectOffsetOnAxis(ap=lidx[slot][:, j:j + 1], axis=0),
                            in_=h1e[slot][:, j, :], in_offset=None,
                            bounds_check=last_node, oob_is_err=False).then_inc(d_sc[slot], 16)

            paired_trips(pool, p2)
            for slot in range(4):
                uses = (TRIPS + 1) // 2 if slot < 2 else TRIPS // 2
                pool.wait_ge(d_sc[slot], 16 * TE * uses)
            pool.sem_inc(p2_done)

            def gather(v, s):
                pool.wait_ge(sidx_ok, v + 1)
                if known(v, 2):
                    pool.wait_ge(catt_ps, v - 1)
                pool.sem_inc(pool_turn)
                for j in range(TE):
                    pool.indirect_dma_start(
                        out=cat[s][:, j, 0:D], out_offset=None, in_=node_table,
                        in_offset=bass.IndirectOffsetOnAxis(ap=sidx[s][:, j:j + 1], axis=0),
                        bounds_check=last_node, oob_is_err=False).then_inc(d_cat[s], 16)

            def scatter(v, s):
                pool.wait_ge(fidx_ok, v + 1)
                pool.wait_ge(res_ok, v + 1)
                pool.sem_inc(pool_turn)
                for j in range(TE):
                    pool.indirect_dma_start(
                        out=out, out_offset=bass.IndirectOffsetOnAxis(ap=fidx[s][:, j:j + 1], axis=0),
                        in_=res[s][:, j, :], in_offset=None,
                        bounds_check=last_node, oob_is_err=False).then_inc(d_fin[s], 16)

            gather(0, 0)
            gather(1, 1)

            def p3(i):
                for s in range(2):
                    v = 2 * i + s
                    if known(v, 2):
                        scatter(v - 2, s)
                    if not (isinstance(i, int) and i == TRIPS - 1):
                        gather(v + 2, s)

            p3(0)
            with pool.Fori(1, TRIPS - 1) as i:
                p3(i)
            p3(TRIPS - 1)
            scatter(UNITS - 2, 0)
            scatter(UNITS - 1, 1)
            for s in range(2):
                pool.wait_ge(d_fin[s], 16 * TE * TRIPS)

        @block.scalar
        def _(act):
            act.wait_ge(d_w, WEIGHT_LOADS)
            act.activation(tanh_b[:, :], tanh_b[:, :], ACT.Tanh).then_inc(c_act, 1)

            def squares_nodes(i, s):
                u = 2 * i + s
                act.wait_ge(ncen_ok, u + 1)
                if known(u, 1):
                    act.wait_ge(nvar_ok, u)
                act.activation(n_sq[:, :, :], h1n[s][:, :, :], ACT.Square, scale=D ** -0.5).then_inc(nsq_ok, 1)

            def squares_edges(i, s):
                u = 2 * i + s
                act.wait_ge(ecen_ok, u + 1)
                if known(u, 1):
                    act.wait_ge(evar_ok, u)
                act.activation(e_sq[:, :, :], e_cen[s][:, :, :], ACT.Square, scale=D ** -0.5).then_inc(esq_ok, 1)
                act.activation(keep[:, ds(u * TE, TE), D:2 * D], xe[s][:, TE:GE, :], ACT.Copy).then_inc(xdst_ok, 1)

            def evacuate(u):
                act.wait_ge(h1t_ps, u + 1)
                if known(u, 1):
                    act.wait_ge(c1_ps, 4 * u)
                act.activation(h1t[:, 0, :], psum[0][:, 0:4 * P], ACT.Copy).then_inc(h1t_ok, 1)
                act.activation(h1t[:, 1, :], psum[1][:, 0:4 * P], ACT.Copy).then_inc(h1t_ok, 1)

            def gelu_hidden(u, quarters):
                for q in quarters:
                    act.wait_ge(c1_ps, 4 * u + q + 1)
                    if q % 2 == 0 and known(u, 1):
                        act.wait_ge(z2_ps, 2 * u - 1 + q // 2)
                    act.activation(c1t[:, q, :], psum[2 + q % 2][0:HC, 0:4 * P], ACT.Gelu,
                                   bias=bc1[:, 0:1]).then_inc(c1_ok, 1)

            def gelu_out(u):
                if known(u, 1):
                    act.wait_ge(g2_ps, u)
                for k in range(2):
                    act.wait_ge(z2_ps, 2 * u + k + 1)
                    act.activation(g2t[:, k, :], psum[4 + k][:, 0:4 * P], ACT.Gelu, bias=bc2[:, 0:1])\
                        .then_inc(g2_ok, 1)

            def p1(i):
                act.wait_ge(nvar_ok, 2 * i + 2)
                act.wait_ge(evar_ok, 2 * i + 2)
                act.activation(std[:, :, :], var[:, :, :], ACT.Sqrt, bias=ln_eps[:, 0:1]).then_inc(std_ok, 1)
                if known(i, 1):
                    gelu_hidden(2 * i - 1, (3,))
                    gelu_out(2 * i - 1)
                evacuate(2 * i)
                more = not (isinstance(i, int) and i == TRIPS - 1)
                gelu_hidden(2 * i, (0, 1, 2, 3))
                if more:
                    squares_nodes(i + 1, 0)
                if more:
                    squares_edges(i + 1, 0)
                evacuate(2 * i + 1)
                gelu_out(2 * i)
                gelu_hidden(2 * i + 1, (0,))
                if more:
                    squares_nodes(i + 1, 1)
                if more:
                    squares_edges(i + 1, 1)
                gelu_hidden(2 * i + 1, (1, 2))

            for s in range(2):
                squares_nodes(0, s)
                squares_edges(0, s)
            p1(0)
            with act.Fori(1, TRIPS - 1) as i:
                p1(i)
            p1(TRIPS - 1)
            gelu_hidden(UNITS - 1, (3,))
            gelu_out(UNITS - 1)

            act.wait_ge(m_step, DIFF_READY)
            act.activation(decay_row[:, :, :], d_row[:, :, :], ACT.Exp).then_inc(m_act, 1)
            act.activation(w_row[:, :, :], z_row[:, :, :], ACT.Exp).then_inc(m_act, 1)

            act.wait_ge(p1_done, 1)

            def tanh_att(i):
                act.wait_ge(att_ok, i + 1)
                if known(i, 1):
                    act.wait_ge(x1_ok, i)
                act.activation(att_th[:, :, :], att_out[:, :, :], ACT.Tanh).then_inc(th_ok, 1)

            def keep_h1(i, parity):
                for s in range(2):
                    u = 2 * i + s
                    act.wait_ge(h1e_ok, u + 1)
                    act.activation(keep[:, ds(u * TE, TE), D:2 * D], h1e[2 * parity + s][:, :, :], ACT.Copy)\
                        .then_inc(h1k_ok, 1)

            def p2(i, parity, n):
                if known(i, 2):
                    keep_h1(i - 1, 1 - parity)
                act.wait_ge(lcen_ok, i + 1)
                if known(i, 1):
                    act.wait_ge(lvar_ok, i)
                act.activation(l_sq[:, :, :], l_cen[:, :, :], ACT.Square, scale=D ** -0.5).then_inc(lsq_ok, 1)
                act.wait_ge(lvar_ok, i + 1)
                if known(i, 1):
                    act.wait_ge(lrstd_ok, i)
                act.activation(l_std[:, :], l_var[:, :], ACT.Sqrt, bias=ln_eps[:, 0:1]).then_inc(lstd_ok, 1)
                act.wait_ge(x1_ok, i + 1)
                act.activation(keep[:, ds(i * 2 * TE, 2 * TE), 0:D], x1_last[:, :, :], ACT.Copy).then_inc(x1k_ok, 1)
                if isinstance(i, int) and i == 0:
                    keep_h1(0, 0)
                if not last_trip(i):
                    tanh_att(i + 1)

            tanh_att(0)
            paired_trips(act, p2)
            keep_h1(TRIPS - 1, (TRIPS - 1) % 2)

            def keep_copy(i, s):
                v = 2 * i + s
                if known(v, 2):
                    act.wait_ge(keptt_ps, v - 1)
                act.activation(kept[s][:, :, :], keep[:, ds(mirror(i, s) * TE, TE), :], ACT.Copy).then_inc(kept_ok, 1)

            def gelu_hidden_e(v):
                act.wait_ge(ce_ps, v + 1)
                if known(v, 1):
                    act.wait_ge(ge_ps, v)
                act.activation(c1e[:, :], psum[5][0:HC, 0:UE], ACT.Gelu, bias=bc1[:, 0:1]).then_inc(ce_ok, 1)

            def gelu_out_e(v):
                act.wait_ge(ge_ps, v + 1)
                if known(v, 1):
                    act.wait_ge(sum_ok, v)
                act.activation(g3t[:, :], psum[6][0:D, 0:UE], ACT.Gelu, bias=bc2[0:D, 0:1]).then_inc(ge_ok, 1)

            act.wait_ge(h1k_ok, UNITS)
            act.wait_ge(x1k_ok, TRIPS)
            keep_copy(0, 0)

            def p3(i):
                for s in range(2):
                    v = 2 * i + s
                    act.wait_ge(catt_ps, v + 1)
                    if known(v, 1):
                        act.wait_ge(m1_ps, v)
                    act.activation(cat_t[:, :], psum[2][0:D + DE, 0:UE], ACT.Copy).then_inc(catt_ok, 1)
                    if known(v, 1):
                        gelu_hidden_e(v - 1)
                    act.wait_ge(m1_ps, v + 1)
                    if known(v, 1):
                        act.wait_ge(m2_ps, v)
                    act.activation(msg_h[:, :], psum[3][0:HM, 0:UE], ACT.Gelu, bias=bm1[:, 0:1]).then_inc(m1_ok, 1)
                    if known(v, 1):
                        gelu_out_e(v - 1)
                    if not (isinstance(i, int) and i == TRIPS - 1 and s == 1):
                        keep_copy(i + s, 1 - s)
                    act.wait_ge(m2_ps, v + 1)
                    if known(v, 1):
                        act.wait_ge(box_ok, v)
                    act.activation(msg[:, :], psum[4][0:D, 0:UE], ACT.Gelu, bias=bm2[:, 0:1]).then_inc(m2_ok, 1)

            p3(0)
            with act.Fori(1, TRIPS - 1) as i:
                p3(i)
            p3(TRIPS - 1)
            gelu_hidden_e(UNITS - 1)
            gelu_out_e(UNITS - 1)

        @block.vector
        def _(dve):
            step = [0]

            def then(ins):
                step[0] += 1
                ins.then_inc(c_step, 1)
                dve.wait_ge(c_step, step[0])

            dve.memset(w0_ext[:, D:D1], 0.0).then_inc(c_step, 1)
            step[0] += 1
            dve.wait_ge(c_step, 1)
            then(dve.memset(w0_ext[D:D1, D:D1], 1.0))
            then(dve.memset(line_m[0:1, 0:1], -BIG))
            then(dve.memset(ln_eps[:, :], LN_EPS))
            dve.wait_ge(d_rows, 16 * (2 + 2 * RB))
            then(dve.tensor_copy(row_dst_f[:, :, :], row_dst[:, :, :]))
            then(dve.tensor_copy(row_src_f[:, :, :], row_src[:, :, :]))
            then(dve.tensor_tensor(same_prev[:, :, :], row_dst_f[:, :, 1:P + 1], row_dst_f[:, :, 0:P], ALU.is_equal))
            then(dve.tensor_tensor(same_next[:, :, :], row_dst_f[:, :, 1:P + 1], row_dst_f[:, :, 2:P + 2], ALU.is_equal))
            assert step[0] == ROWS_READY
            then(dve.tensor_scalar(pen[:, :, :], same_prev[:, :, :], -1.0, BIG, ALU.add, ALU.mult))
            then(dve.tensor_reduce(pen_min[:, :], pen[:, :, :], AX.X, ALU.min))
            dve.wait_ge(c_pe, 1)
            idx_v = gather_idx[:, :, :]
            then(dve.tensor_copy(idx_v[:, :, 0:TE], psum[0][0:P, 0:ET].rearrange("p (u j) -> p u j", j=TE)))
            then(dve.tensor_copy(idx_v[:, :, TE:GE], psum[0][0:P, 256:256 + ET].rearrange("p (u j) -> p u j", j=TE)))

            def stage_idx(u, s):
                dve.tensor_copy(idx_now[s][:, :], gather_idx[:, ds(u, 1), :].rearrange("p a g -> p (a g)"))\
                    .then_inc(idx_ok, 1)

            stage_idx(0, 0)
            stage_idx(1, 1)
            then(dve.tensor_copy(dst_f[:, :], psum[0][0:P, 256:256 + ET]))
            for psum_at, flag, tmp, idx in ((256, last_f, tmp_l, last_idx), (0, first_f, tmp_f, first_idx)):
                then(dve.tensor_scalar(flag[:, :], psum[1][0:P, psum_at:psum_at + ET], -1.0, 1.0, ALU.mult, ALU.add))
                then(dve.tensor_scalar(tmp[:, :], dst_f[:, :], -SKIP, None, ALU.add))
                then(dve.tensor_tensor(tmp[:, :], tmp[:, :], flag[:, :], ALU.mult))
                then(dve.tensor_scalar(idx[:, :], tmp[:, :], SKIP, None, ALU.add))
            dve.wait_ge(c_pe, 2)
            dve.wait_ge(d_w, WEIGHT_LOADS)
            then(dve.tensor_copy(w0_t[:, :], psum[2][0:D, 0:D]))
            then(dve.tensor_copy(att_rep[:, :, :], bcast(att_col[:, :], [D, 2, 128], 2)))
            assert step[0] == ATT_READY
            dve.wait_ge(c_pe, 3)
            for g in range(2):
                then(dve.tensor_copy(att_vec[:, g * TE:(g + 1) * TE, :],
                                     bcast(psum[2][0:P, 64 + g * D:64 + (g + 1) * D], [P, TE, D], 1)))
            dve.wait_ge(c_act, 1)

            def sums(i, s):
                u = 2 * i + s
                dve.wait_ge(d_xe[s], 16 * GE * (i + 1))
                dve.tensor_reduce(e_sum[s][:, :], xe[s][:, :, :], AX.X, ALU.add).then_inc(esum_ok, 1)
                if s == 0 and known(i, 2):
                    finish_nodes(i - 2, 1)
                if s == 0:
                    dve.wait_ge(d_xn[s], 32 * (i + 1))
                    if known(i, 1):
                        dve.wait_ge(s1n_ok[s], i)
                    dve.tensor_tensor(x1n[s][:, :, :], xn[s][:, :, :], bcast(tanh_b[:, :], [P, TN, D], 1),
                                      ALU.add).then_inc(nx1_ok[s], 1)
                dve.wait_ge(nx1_ok[s], i + 1)
                dve.tensor_reduce(n_sum[s][:, :], x1n[s][:, :, :], AX.X, ALU.add).then_inc(nsum_ok, 1)

            def centre(i, s):
                u = 2 * i + s
                dve.wait_ge(esum_ok, u + 1)
                dve.scalar_tensor_tensor(out=e_cen[s][:, :, :], in0=bcast(e_sum[s][:, :], [P, GE, D], 2),
                                         scalar=-1.0 / D, in1=xe[s][:, :, :],
                                         op0=ALU.mult, op1=ALU.add).then_inc(ecen_ok, 1)
                if known(u, 2):
                    dve.wait_ge(d_tab[s], 32 * i)
                    dve.wait_ge(h1t_ps, u - 1)
                    dve.wait_ge(s1n_ok[s], i)
                dve.wait_ge(nsum_ok, u + 1)
                dve.scalar_tensor_tensor(out=h1n[s][:, :, :], in0=bcast(n_sum[s][:, :], [P, TN, D], 2),
                                         scalar=-1.0 / D, in1=x1n[s][:, :, :],
                                         op0=ALU.mult, op1=ALU.add).then_inc(ncen_ok, 1)
                if not (isinstance(i, int) and i == TRIPS - 1):
                    stage_idx(u + 2, s)

            def variances(i, s):
                u = 2 * i + s
                dve.wait_ge(nsq_ok, u + 1)
                if s == 0 and known(i, 1):
                    dve.wait_ge(std_ok, i)
                dve.tensor_reduce(var[:, s, 0:TN], n_sq[:, :, :], AX.X, ALU.add).then_inc(nvar_ok, 1)
                dve.wait_ge(esq_ok, u + 1)
                dve.tensor_reduce(var[:, s, TN:], e_sq[:, :, :], AX.X, ALU.add).then_inc(evar_ok, 1)

            def dots(u, s):
                dve.wait_ge(ecen_ok, u + 1)
                if known(u, 1):
                    dve.wait_ge(edot_ok, u)
                dve.scalar_tensor_tensor(out=e_prod[:, :, :], in0=e_cen[s][:, :, :], scalar=0.0,
                                         in1=att_vec[:, :, :], op0=ALU.max, op1=ALU.mult).then_inc(eprod_ok, 1)
                dve.wait_ge(eprod_ok, u + 1)
                dve.tensor_reduce(e_dot[s][:, :], e_prod[:, :, :], AX.X, ALU.add).then_inc(edot_ok, 1)

            def normalise(i, s):
                u = 2 * i + s
                dve.scalar_tensor_tensor(out=h1n[s][:, :, :], in0=h1n[s][:, :, :], scalar=0.0,
                                         in1=bcast(rstd[:, s, 0:TN], [P, TN, D], 2),
                                         op0=ALU.max, op1=ALU.mult).then_inc(h1n_ok, 1)
                dve.wait_ge(edot_ok, u + 1)
                if known(u, 1):
                    dve.wait_ge(logit_ok, u)
                dve.tensor_tensor(e_sc[:, :], e_dot[s][:, :], rstd[:, s, TN:], ALU.mult).then_inc(esc_ok, 1)
                dve.scalar_tensor_tensor(out=keep[:, ds(u * TE, TE), 0:D], in0=e_cen[s][:, 0:TE, :], scalar=0.0,
                                         in1=bcast(rstd[:, s, TN:TN + TE], [P, TE, D], 2),
                                         op0=ALU.max, op1=ALU.mult).then_inc(keeph_ok, 1)
                dve.wait_ge(esc_ok, u + 1)
                dve.tensor_tensor(logit[:, ds(u * TE, TE)], e_sc[:, 0:TE], e_sc[:, TE:GE], ALU.add)\
                    .then_inc(logit_ok, 1)
                if s == 0:
                    dve.wait_ge(h1n_ok, u + 1)
                    dve.tensor_tensor(s1n[s][:, :, :], x1n[s][:, :, :], h1n[s][:, :, :], ALU.add)\
                        .then_inc(s1n_ok[s], 1)

            def p1(i):
                sums(i, 0)
                centre(i, 0)
                sums(i, 1)
                variances(i, 0)
                centre(i, 1)
                dots(2 * i, 0)
                variances(i, 1)
                dots(2 * i + 1, 1)
                if known(i, 1):
                    finish_nodes(i - 1, 0)
                dve.wait_ge(std_ok, i + 1)
                dve.reciprocal(rstd[:, :, :], std[:, :, :]).then_inc(rstd_ok, 1)
                dve.wait_ge(rstd_ok, i + 1)
                if known(i, 1):
                    dve.wait_ge(resn_ok, 2 * i - 1)
                normalise(i, 0)
                normalise(i, 1)

            def finish_nodes(i, s):
                u = 2 * i + s
                dve.wait_ge(g2_ps, u + 1)
                dve.wait_ge(s1n_ok[s], i + 1)
                if known(i, 1):
                    dve.wait_ge(d_res[s], 32 * i)
                dve.tensor_tensor(resn[s][:, :, :].rearrange("p (b j) d -> p b (j d)", b=2), psum_all[0:P, 6:8, :],
                                  s1n[s][:, :, :].rearrange("p (b j) d -> p b (j d)", b=2), ALU.add)\
                    .then_inc(resn_ok, 1)

            for i in range(2):
                p1(i)
            with dve.Fori(2, TRIPS - 1) as i:
                p1(i)
            p1(TRIPS - 1)
            finish_nodes(TRIPS - 2, 1)

            mark = [0]

            def then_m(ins):
                mark[0] += 1
                ins.then_inc(m_step, 1)
                dve.wait_ge(m_step, mark[0])

            def by_row(bank):
                return psum[bank][0:RR, 0:RB * P].rearrange("r (b p) -> r b p", p=P)

            dve.wait_ge(m_pe, 1)
            then_m(dve.tensor_copy(z_row[:, :, :], by_row(0)))
            then_m(dve.scalar_tensor_tensor(out=e_row[:, :, :], in0=z_row[:, :, :], scalar=SLOPE,
                                            in1=z_row[:, :, :], op0=ALU.mult, op1=ALU.max))
            for b in range(RB):
                then_m(dve.tensor_tensor_scan(m_row[:, b, :], pen[:, b, :], e_row[:, b, :], -BIG, ALU.add, ALU.max))
            assert mark[0] == ROW_MAX_READY
            dve.wait_ge(m_pe, 2)
            then_m(dve.tensor_copy(line[0:1, :], psum[1][0:1, 0:2 * ET]))
            then_m(dve.tensor_tensor_scan(line_m[0:1, 1:ET + 1], line[0:1, ET:2 * ET], line[0:1, 0:ET], -BIG,
                                          ALU.add, ALU.max))
            assert mark[0] == LINE_READY
            dve.wait_ge(m_pe, 3)
            then_m(dve.tensor_copy(m_run[:, :, 0], psum[0][0:RR, 0:RB]))
            for b in range(RB):
                then_m(dve.tensor_tensor_scan(m_run[:, b, 1:P + 1], pen[:, b, :], e_row[:, b, :], m_run[:, b, 0:1],
                                              ALU.add, ALU.max))
            then_m(dve.tensor_tensor(d_row[:, :, :], m_run[:, :, 0:P], m_run[:, :, 1:P + 1], ALU.subtract))
            then_m(dve.tensor_scalar(d_row[:, :, :], d_row[:, :, :], 0.0, None, ALU.min))
            then_m(dve.tensor_tensor(z_row[:, :, :], e_row[:, :, :], m_run[:, :, 1:P + 1], ALU.subtract))
            assert mark[0] == DIFF_READY
            finish_nodes(TRIPS - 1, 0)
            finish_nodes(TRIPS - 1, 1)
            dve.wait_ge(m_act, 1)
            then_m(dve.tensor_tensor(decay_row[:, :, :], decay_row[:, :, :], same_prev[:, :, :], ALU.mult))
            assert mark[0] == DECAY_READY
            dve.wait_ge(m_pe, 4)
            then_m(dve.tensor_copy(weight[:, :], psum[1][0:P, 0:ET]))
            assert mark[0] == SM_DONE

            dve.wait_ge(p1_done, 1)
            dve.memset(acc[1][:, UE - 1:UE], 0.0).then_inc(p2_ready, 1)
            dve.wait_ge(p2_ready, 1)

            def weigh(i):
                if known(i, 1):
                    dve.wait_ge(wht_ps, 2 * i)
                t = ds(i * 2 * TE, 2 * TE)
                dve.tensor_tensor(wh[:, :, 0:D], keep[:, t, 0:D], bcast(weight[:, t], [P, 2 * TE, D], 2),
                                  ALU.mult).then_inc(wh_ok, 1)
                dve.tensor_copy(wh[:, :, D], weight[:, t]).then_inc(whw_ok, 1)

            def take_last(i):
                t = ds(i * 2 * TE, 2 * TE)
                if known(i, 1):
                    dve.wait_ge(x1_ok, i)
                dve.tensor_tensor(x_last[:, :, :], keep[:, t, D:2 * D], bcast(last_f[:, t], [P, 2 * TE, D], 2),
                                  ALU.mult).then_inc(xlast_ok, 1)

            def running_sums(i):
                for s in range(2):
                    u = 2 * i + s
                    dve.wait_ge(wht_ps, u + 1)
                    dve.wait_ge(d_dec[s], 16 * (i + 1))
                    if known(u, 1):
                        dve.wait_ge(acc_ok, u)
                    if known(u, 2):
                        dve.wait_ge(num_ps, u - 1)
                    dve.tensor_tensor_scan(acc[s][:, :], decay[s][:, :], psum[s][0:D1, 0:UE],
                                           acc[1 - s][:, UE - 1:UE], ALU.mult, ALU.add).then_inc(acc_ok, 1)

            def attention(i):
                t = ds(i * 2 * TE, 2 * TE)
                dve.wait_ge(num_ps, 2 * i + 2)
                num = psum_all[0:P, 2:4, 0:TE * D1].rearrange("p b (j d) -> p b j d", d=D1)
                dve.tensor_scalar(den_eps[:, :].rearrange("p (b j) -> p b j", b=2), num[:, :, :, D], SM_EPS, None,
                                  ALU.add).then_inc(dene_ok, 1)
                dve.wait_ge(dene_ok, i + 1)
                dve.reciprocal(den_inv[:, :], den_eps[:, :]).then_inc(deni_ok, 1)
                dve.wait_ge(deni_ok, i + 1)
                dve.tensor_tensor(den_last[:, :], den_inv[:, :], last_f[:, t], ALU.mult).then_inc(denl_ok, 1)
                dve.wait_ge(denl_ok, i + 1)
                for s in range(2):
                    ins = dve.tensor_tensor(att_out[:, s * TE:(s + 1) * TE, :], num[:, s, :, 0:D],
                                            bcast(den_last[:, s * TE:(s + 1) * TE], [P, TE, D], 2), ALU.mult)
                ins.then_inc(att_ok, 1)

            def h1_last(i, parity, n):
                dve.wait_ge(lstd_ok, i + 1)
                dve.reciprocal(l_rstd[:, :], l_std[:, :]).then_inc(lrstd_ok, 1)
                for s in range(2):
                    if known(n, 1):
                        dve.wait_ge(d_sc[2 * parity + s], 16 * TE * n)
                    dve.tensor_copy(lidx[2 * parity + s][:, :], last_idx[:, ds(2 * i * TE + s * TE, TE)])\
                        .then_inc(lidx_ok, 1)
                dve.wait_ge(lrstd_ok, i + 1)
                for s in range(2):
                    if known(i, 2):
                        dve.wait_ge(h1k_ok, 2 * i - 3 + s)
                    dve.scalar_tensor_tensor(out=h1e[2 * parity + s][:, :, :], in0=l_cen[:, s * TE:(s + 1) * TE, :],
                                             scalar=0.0, in1=bcast(l_rstd[:, s * TE:(s + 1) * TE], [P, TE, D], 2),
                                             op0=ALU.max, op1=ALU.mult).then_inc(h1e_ok, 1)

            def p2(i, parity, n):
                if not last_trip(i):
                    running_sums(i + 1)
                if known(i, 2):
                    h1_last(i - 1, 1 - parity, n - 1 + parity)
                dve.wait_ge(th_ok, i + 1)
                dve.wait_ge(xlast_ok, i + 1)
                if known(i, 1):
                    dve.wait_ge(x1k_ok, i)
                dve.tensor_tensor(x1_last[:, :, :], x_last[:, :, :], att_th[:, :, :], ALU.add).then_inc(x1_ok, 1)
                dve.wait_ge(x1_ok, i + 1)
                dve.tensor_reduce(l_sum[:, :], x1_last[:, :, :], AX.X, ALU.add).then_inc(lsum_ok, 1)
                if known(i, 1):
                    dve.wait_ge(h1e_ok, 2 * i)
                dve.wait_ge(lsum_ok, i + 1)
                dve.scalar_tensor_tensor(out=l_cen[:, :, :], in0=bcast(l_sum[:, :], [P, 2 * TE, D], 2),
                                         scalar=-1.0 / D, in1=x1_last[:, :, :],
                                         op0=ALU.mult, op1=ALU.add).then_inc(lcen_ok, 1)
                if not (isinstance(i, int) and i >= TRIPS - 2):
                    weigh(i + 2)
                dve.wait_ge(lsq_ok, i + 1)
                dve.tensor_reduce(l_var[:, :], l_sq[:, :, :], AX.X, ALU.add).then_inc(lvar_ok, 1)
                if not last_trip(i):
                    take_last(i + 1)
                if isinstance(i, int) and i == 0:
                    h1_last(0, 0, 0)
                if not last_trip(i):
                    attention(i + 1)

            weigh(0)
            take_last(0)
            running_sums(0)
            weigh(1)
            attention(0)
            paired_trips(dve, p2)
            h1_last(TRIPS - 1, (TRIPS - 1) % 2, (TRIPS - 1) // 2)

            def stage_src(i, s):
                v = 2 * i + s
                if known(v, 2):
                    dve.wait_ge(d_cat[s], 16 * TE * i)
                dve.tensor_copy(sidx[s][:, :],
                                gather_idx[:, ds(mirror(i, s), 1), 0:TE].rearrange("p a g -> p (a g)"))\
                    .then_inc(sidx_ok, 1)

            def stage_first(i, s):
                v = 2 * i + s
                if known(v, 2):
                    dve.wait_ge(d_fin[s], 16 * TE * i)
                dve.tensor_copy(fidx[s][:, :], first_idx[:, ds(mirror(i, s) * TE, TE)]).then_inc(fidx_ok, 1)

            def box_sums(v, s):
                dve.wait_ge(m2_ok, v + 1)
                if known(v, 1):
                    dve.wait_ge(box_ok, v)
                if known(v, 2):
                    dve.wait_ge(ce_ps, v - 1)
                dve.tensor_tensor_scan(pair[s][0:D, ::-1], same[s][0:D, ::-1], msg[:, ::-1],
                                       pair[1 - s][0:D, 0:1], ALU.mult, ALU.add).then_inc(box_ok, 1)

            def fill_back(i, s):
                v = 2 * i + s
                dve.wait_ge(keptt_ps, v + 1)
                dve.wait_ge(d_same[s], 16 * (i + 1))
                if known(v, 1):
                    dve.wait_ge(fill_ok, v)
                if known(v, 2):
                    dve.wait_ge(fin_ps, v - 1)
                dve.tensor_tensor_scan(fill[s][:, ::-1], same[s][:, ::-1], psum[s][:, UE - 1::-1],
                                       fill[1 - s][:, 0:1], ALU.mult, ALU.add).then_inc(fill_ok, 1)
                if known(v, 1):
                    dve.wait_ge(pairh_ok, v)
                if known(v, 2):
                    dve.wait_ge(ce_ps, v - 1)
                dve.tensor_tensor_scan(pair[s][D:2 * D, ::-1], same[s][D:2 * D, ::-1], psum[s][D:2 * D, UE - 1::-1],
                                       pair[1 - s][D:2 * D, 0:1], ALU.mult, ALU.add).then_inc(pairh_ok, 1)

            def add_out(v, s):
                dve.wait_ge(ge_ok, v + 1)
                dve.wait_ge(fill_ok, v + 1 if isinstance(v, int) and v == UNITS - 1 else v + 2)
                dve.tensor_tensor(fill[s][0:D, :], fill[s][0:D, :], g3t[:, :], ALU.add).then_inc(sum_ok, 1)

            def finish_edges(i, s):
                v = 2 * i + s
                dve.wait_ge(fin_ps, v + 1)
                stage_first(i, s)
                fin = psum[7][0:P, :].rearrange("p (j d) -> p j d", d=2 * D)
                if known(v, 1):
                    dve.wait_ge(res_ok, v)
                dve.tensor_copy(h1_row[:, :, :], fin[:, :, D:2 * D]).then_inc(h1row_ok, 1)
                dve.wait_ge(h1row_ok, v + 1)
                dve.tensor_tensor(res[s][:, :, :], fin[:, :, 0:D], h1_row[:, :, :], ALU.add).then_inc(res_ok, 1)

            dve.memset(fill[1][:, 0:1], 0.0).then_inc(p2_ready, 1)
            dve.memset(pair[1][:, 0:1], 0.0).then_inc(p2_ready, 1)
            dve.wait_ge(p2_ready, 3)
            stage_src(0, 0)
            stage_src(0, 1)

            def p3(i):
                for s in range(2):
                    v = 2 * i + s
                    if known(v, 1):
                        box_sums(v - 1, 1 - s)
                    if known(v, 2):
                        finish_edges(i - 1, s)
                    fill_back(i, s)
                    if not (isinstance(i, int) and i == TRIPS - 1):
                        stage_src(i + 1, s)
                    if known(v, 1):
                        add_out(v - 1, 1 - s)

            p3(0)
            with dve.Fori(1, TRIPS - 1) as i:
                p3(i)
            p3(TRIPS - 1)
            box_sums(UNITS - 1, 1)
            finish_edges(TRIPS - 1, 0)
            add_out(UNITS - 1, 1)
            finish_edges(TRIPS - 1, 1)

        @block.tensor
        def _(pe):
            pe.wait_ge(ident_ok, 1)
            pe.wait_ge(c_step, ROWS_READY)
            for b in range(RB):
                pe.transpose(psum[0][0:P, b * RR:(b + 1) * RR], row_src_f[:, b, :], ident[0:RR, 0:RR])
                pe.transpose(psum[0][0:P, 256 + b * RR:256 + (b + 1) * RR], row_dst_f[:, b, 1:P + 1], ident[0:RR, 0:RR])
                pe.transpose(psum[1][0:P, b * RR:(b + 1) * RR], same_prev[:, b, :], ident[0:RR, 0:RR])
                last = pe.transpose(psum[1][0:P, 256 + b * RR:256 + (b + 1) * RR], same_next[:, b, :], ident[0:RR, 0:RR])
            last.then_inc(c_pe, 1)
            pe.wait_ge(d_w, WEIGHT_LOADS)
            pe.transpose(psum[2][0:D, 0:D], w0_ext[0:D, 0:D], ident[0:D, 0:D]).then_inc(c_pe, 1)
            pe.wait_ge(c_step, ATT_READY)
            for g in range(2):
                last = pe.matmul(psum[2][:, 64 + g * D:64 + (g + 1) * D], att_rep[:, g, :], w0_t[:, :],
                                 start=True, stop=True)
            last.then_inc(c_pe, 1)

            def out_layer(u):
                for k in range(2):
                    if known(u, 1):
                        pe.wait_ge(g2_ok, 2 * u - 1 + k)
                    for q in range(2):
                        pe.wait_ge(c1_ok, 4 * u + 2 * k + q + 1)
                        last = pe.matmul(psum[4 + k][q * D:(q + 1) * D, 0:4 * P], wc2[:, :],
                                         c1t[:, 2 * k + q, :], start=True, stop=True)
                    last.then_inc(z2_ps, 1)

            def turn_back(u):
                if known(u, 1):
                    pe.wait_ge(resn_ok, u)
                for c in range(TN // 2):
                    if c % 4 == 0:
                        pe.wait_ge(g2_ok, 2 * u + c // 4 + 1)
                    last = pe.transpose(psum[6 + c // 4][0:P, (c % 4) * 2 * D:(c % 4 + 1) * 2 * D],
                                        g2t[:, c // 4, (c % 4) * P:(c % 4 + 1) * P], ident[:, :])
                last.then_inc(g2_ps, 1)

            def turn(u, s):
                pe.wait_ge(h1n_ok, u + 1)
                if known(u, 1):
                    pe.wait_ge(h1t_ok, 2 * u)
                for c in range(TN // 2):
                    last = pe.transpose(psum[c // 4][:, (c % 4) * P:(c % 4 + 1) * P],
                                        h1n[s][:, 2 * c:2 * c + 2, :].rearrange("p j d -> p (j d)"),
                                        ident[0:P, 0:P])
                last.then_inc(h1t_ps, 1)

            def hidden_layer(u, halves=(0, 1)):
                for k in halves:
                    pe.wait_ge(h1t_ok, 2 * u + k + 1)
                    for q in range(2):
                        if known(4 * u + 2 * k + q, 2):
                            pe.wait_ge(c1_ok, 4 * u + 2 * k + q - 1)
                        pe.matmul(psum[2 + q][0:HC, 0:4 * P], wc1_bh[D:2 * D, :] if q else wc1_h[:, :],
                                  h1t[q * D:(q + 1) * D, k, :], start=True, stop=True).then_inc(c1_ps, 1)

            def p1(i):
                turn(2 * i, 0)
                if known(i, 1):
                    turn_back(2 * i - 1)
                hidden_layer(2 * i)
                turn(2 * i + 1, 1)
                out_layer(2 * i)
                hidden_layer(2 * i + 1, (0,))
                if last_trip(i):
                    logits_by_row()
                turn_back(2 * i)
                if last_trip(i):
                    row_ends()
                hidden_layer(2 * i + 1, (1,))
                if last_trip(i):
                    max_before_rows()
                out_layer(2 * i + 1)

            pe.wait_ge(c_step, CONST_READY)
            def logits_by_row():
                pe.wait_ge(logit_ok, UNITS)
                pe.wait_ge(h1t_ok, 2 * UNITS)
                for b in range(RB):
                    last = pe.transpose(psum[0][0:RR, b * P:(b + 1) * P], logit[:, b * RR:(b + 1) * RR],
                                        ident[0:P, 0:P])
                last.then_inc(m_pe, 1)

            def row_ends():
                pe.wait_ge(m_step, ROW_MAX_READY)
                for b in range(RB):
                    pe.transpose(psum[1][0:1, b * RR:(b + 1) * RR], m_row[:, b, P - 1:P], ident[0:RR, 0:RR])
                    last = pe.transpose(psum[1][0:1, ET + b * RR:ET + (b + 1) * RR], pen_min[:, b:b + 1],
                                        ident[0:RR, 0:RR])
                last.then_inc(m_pe, 1)

            def max_before_rows():
                pe.wait_ge(m_step, LINE_READY)
                for b in range(RB):
                    last = pe.transpose(psum[0][0:RR, b:b + 1], line_m[0:1, b * RR:(b + 1) * RR], ident[0:1, 0:1])
                last.then_inc(m_pe, 1)

            p1(0)
            with pe.Fori(1, TRIPS - 1) as i:
                p1(i)
            p1(TRIPS - 1)
            turn_back(UNITS - 1)

            pe.wait_ge(m_act, 2)
            for b in range(RB):
                last = pe.transpose(psum[1][0:P, b * RR:(b + 1) * RR], w_row[:, b, :], ident[0:RR, 0:RR])
            last.then_inc(m_pe, 1)

            pe.wait_ge(p1_done, 1)

            def p2(i):
                for s in range(2):
                    u = 2 * i + s
                    if s == 0:
                        pe.wait_ge(wh_ok, i + 1)
                        pe.wait_ge(whw_ok, i + 1)
                    if known(u, 2):
                        pe.wait_ge(acc_ok, u - 1)
                    for j in range(TE):
                        last = pe.transpose(psum[s][0:D1, j * P:(j + 1) * P], wh[:, s * TE + j, :], ident[0:P, 0:P])
                    last.then_inc(wht_ps, 1)
                for s in range(2):
                    u = 2 * i + s
                    pe.wait_ge(acc_ok, u + 1)
                    if s == 0 and known(i, 1):
                        pe.wait_ge(att_ok, i)
                    for j in range(TE):
                        last = pe.matmul(psum[2 + s][0:P, j * D1:(j + 1) * D1], acc[s][:, j * P:(j + 1) * P],
                                         w0_ext[:, :], start=True, stop=True)
                    last.then_inc(num_ps, 1)

            trips(pe, p2)

            def turn_edges(v, s, i):
                pe.wait_ge(kept_ok, v + 1)
                if known(v, 2):
                    pe.wait_ge(fill_ok, v - 1)
                for j in range(TE):
                    last = pe.transpose(psum[s][:, j * P:(j + 1) * P], kept[s][:, j, :], ident[0:P, 0:P])
                last.then_inc(keptt_ps, 1)
                pe.wait_ge(d_cat[s], 16 * TE * (i + 1))
                pe.wait_ge(d_ea[s], 16 * (i + 1))
                if known(v, 1):
                    pe.wait_ge(catt_ok, v)
                for j in range(TE):
                    last = pe.transpose(psum[2][0:D + DE, j * P:(j + 1) * P], cat[s][:, j, :], ident[0:P, 0:P])
                last.then_inc(catt_ps, 1)

            def node_hidden(v, s):
                pe.wait_ge(box_ok, v + 1)
                if known(v, 1):
                    pe.wait_ge(ce_ok, v)
                pe.matmul(psum[5][0:HC, 0:UE], wc1_bh[:, :], pair[s][:, :], start=True, stop=True).then_inc(ce_ps, 1)

            def node_out(v):
                pe.wait_ge(ce_ok, v + 1)
                if known(v, 1):
                    pe.wait_ge(ge_ok, v)
                pe.matmul(psum[6][0:D, 0:UE], wc2[:, :], c1e[:, :], start=True, stop=True).then_inc(ge_ps, 1)

            def turn_back_edges(v, s):
                pe.wait_ge(sum_ok, v + 1)
                if known(v, 1):
                    pe.wait_ge(res_ok, v)
                for j in range(TE):
                    last = pe.transpose(psum[7][0:P, j * 2 * D:(j + 1) * 2 * D], fill[s][:, j * P:(j + 1) * P],
                                        ident[:, :])
                last.then_inc(fin_ps, 1)

            def p3(i):
                for s in range(2):
                    v = 2 * i + s
                    if known(v, 2):
                        turn_back_edges(v - 2, s)
                    turn_edges(v, s, i)
                    if known(v, 1):
                        node_hidden(v - 1, 1 - s)
                    pe.wait_ge(catt_ok, v + 1)
                    pe.wait_ge(fill_ok, v + 1)
                    pe.wait_ge(pairh_ok, v + 1)
                    if known(v, 1):
                        pe.wait_ge(m1_ok, v)
                    pe.matmul(psum[3][0:HM, 0:UE], wm1_src[:, :], cat_t[:, :], start=True, stop=False)
                    pe.matmul(psum[3][0:HM, 0:UE], wm1_dst[D:2 * D, :], pair[s][D:2 * D, :], start=False, stop=True)\
                        .then_inc(m1_ps, 1)
                    if known(v, 1):
                        node_out(v - 1)
                    pe.wait_ge(m1_ok, v + 1)
                    if known(v, 1):
                        pe.wait_ge(m2_ok, v)
                    pe.matmul(psum[4][0:D, 0:UE], wm2[:, :], msg_h[:, :], start=True, stop=True).then_inc(m2_ps, 1)

            trips(pe, p3)
            turn_back_edges(UNITS - 2, 0)
            node_hidden(UNITS - 1, 1)
            node_out(UNITS - 1)
            turn_back_edges(UNITS - 1, 1)


WEIGHT_LOADS = 16 * 18
ROWS_READY = 8
ATT_READY = 23
CONST_READY = 25
ROW_MAX_READY = 4
LINE_READY = 6
DIFF_READY = 12
DECAY_READY = 13
SM_DONE = 14

_INS = ['x', 'src', 'dst', 'edge_attr_32', 'L0_gnn_W', 'L0_gnn_att_src', 'L0_gnn_att_dst', 'L0_gnn_bias',
        'L1_gnn_W_m1', 'L1_gnn_b_m1', 'L1_gnn_W_m2', 'L1_gnn_b_m2', 'L1_gnn_W_c1', 'L1_gnn_b_c1', 'L1_gnn_W_c2',
        'L1_gnn_b_c2']
_OUTS = [((100000, 64), 'float32')]


def kernel(**inputs):
    import numpy as _np
    import concourse.bacc as _bacc
    from concourse import mybir as _mybir
    from concourse.bass_utils import run_bass_kernel_spmd as _run

    nc = _bacc.Bacc("TRN2", target_bir_lowering=False, num_devices=1)
    arrays, args = {}, []
    for name in _INS:
        a = _np.ascontiguousarray(inputs[name])
        arrays[f"in_{name}_dram"] = a
        args.append(nc.dram_tensor(f"in_{name}_dram", a.shape, _mybir.dt.from_np(a.dtype), kind="ExternalInput").ap())
    for i, (shape, dtype) in enumerate(_OUTS):
        dt = _mybir.dt.from_np(_np.dtype(dtype))
        args.append(nc.dram_tensor(f"out_{i}_dram", shape, dt, kind="ExternalOutput").ap())
    gnn_two_layer_kernel(nc, *args)
    r = _run(nc, [arrays], core_ids=[0])
    return r.results[0]["out_0_dram"]
```
